# Optimizing a Trainium2 kernel written in Bass

```python
import numpy as np
import jax
import jax.numpy as jnp

def _softmax(x, axis=-1):
    return jax.nn.softmax(x, axis=axis)

def _gelu(x):
    return jax.nn.gelu(x, approximate=True)

def _silu(x):
    return jax.nn.silu(x)

def _sigmoid(x):
    return jax.nn.sigmoid(x)

def _layernorm(x, axis=-1, eps=1e-05):
    m = jnp.mean(x, axis=axis, keepdims=True)
    v = jnp.var(x, axis=axis, keepdims=True)
    return (x - m) / jnp.sqrt(v + eps)

def _scatter_add(tgt, idx, src, axis=0):
    return tgt.at[idx].add(src)

def _segment_sum(src, seg, n):
    return jax.ops.segment_sum(src, seg, n)
kernel_name = 'mk_gnn_resnorm_d2_gnn_r32_619fd0'

def setup_inputs(seed: int=0):
    np.random.seed(seed)
    _w = jnp.asarray

    def _rec_inputs():
        import jax
        import jax.numpy as jnp
        _gk = jax.random.key(seed)
        x = -0.000202 + 1 * jax.random.normal(jax.random.fold_in(_gk, 1), (3125, 128), jnp.float32)
        src = jax.random.randint(jax.random.fold_in(_gk, 2), (100000,), 0, 3125, jnp.int32)
        dst = jax.random.randint(jax.random.fold_in(_gk, 3), (100000,), 0, 3125, jnp.int32)
        _o = jnp.argsort(dst, stable=True)
        src = src[_o]
        dst = dst[_o]
        edge_weight = jax.random.uniform(jax.random.fold_in(_gk, 13), (100000,), jnp.float32, 0.0, 1)
        return (x, src, dst, edge_weight)
    x, src, dst, edge_weight = _rec_inputs()

    def _L0_gnn_setup():
        import jax, jax.numpy as jnp
        import numpy as np
        N_NODES = 50000
        N_EDGES = 25000
        HID = 128
        key = jax.random.key(seed)
        ks = jax.random.split(key, 10)
        s_msg = 1.0 / np.sqrt(2 * HID + 1)
        s_u1 = 1.0 / np.sqrt(2 * HID)
        s_u2 = 1.0 / np.sqrt(HID)
        return {'z': jax.random.normal(ks[0], (N_NODES, HID), dtype=jnp.float32), 'edge_weight': jax.random.uniform(ks[1], (N_EDGES,), dtype=jnp.float32), 'edge_src': jax.random.randint(ks[2], (N_EDGES,), 0, N_NODES), 'edge_dst': jax.random.randint(ks[3], (N_EDGES,), 0, N_NODES), 'Wm': jax.random.normal(ks[4], (2 * HID + 1, HID), dtype=jnp.float32) * s_msg, 'bm': jax.random.normal(ks[5], (HID,), dtype=jnp.float32) * s_msg, 'W1': jax.random.normal(ks[6], (2 * HID, HID), dtype=jnp.float32) * s_u1, 'b1': jax.random.normal(ks[7], (HID,), dtype=jnp.float32) * s_u1, 'W2': jax.random.normal(ks[8], (HID, HID), dtype=jnp.float32) * s_u2, 'b2': jax.random.normal(ks[9], (HID,), dtype=jnp.float32) * s_u2}
    _L0_gnn_all = _L0_gnn_setup()
    _L0_gnn_in = {k: v for k, v in _L0_gnn_all.items() if k in ('Wm', 'bm', 'W1', 'b1', 'W2', 'b2')}
    del _L0_gnn_all

    def _L1_gnn_setup():
        import jax, jax.numpy as jnp
        import numpy as np
        N_NODES = 50000
        N_EDGES = 25000
        IN_CH, HID_CH, OUT_CH = (128, 256, 128)

        def _glorot(key, shape):
            fan_in, fan_out = (shape[1], shape[0])
            lim = float(np.sqrt(6.0 / (fan_in + fan_out)))
            return jax.random.uniform(key, shape, jnp.float32, -lim, lim)

        def _sage_conv(x, src, dst, Wl, bl, Wr, n_nodes):
            msg = x[src]
            agg = jax.ops.segment_sum(msg, dst, num_segments=n_nodes)
            deg = jax.ops.segment_sum(jnp.ones((src.shape[0],), x.dtype), dst, num_segments=n_nodes)
            mean = agg / jnp.maximum(deg, 1.0)[:, None]
            return mean @ Wl.T + bl + x @ Wr.T
        key = jax.random.key(seed)
        ks = jax.random.split(key, 8)
        x = jax.random.normal(ks[0], (N_NODES, IN_CH), jnp.float32)
        edge_index = jax.random.randint(ks[1], (2, N_EDGES), 0, N_NODES, jnp.int64)
        return {'x': x, 'edge_index': edge_index, 'W1l': _glorot(ks[2], (HID_CH, IN_CH)), 'b1l': jnp.zeros((HID_CH,), jnp.float32), 'W1r': _glorot(ks[3], (HID_CH, IN_CH)), 'W2l': _glorot(ks[4], (OUT_CH, HID_CH)), 'b2l': jnp.zeros((OUT_CH,), jnp.float32), 'W2r': _glorot(ks[5], (OUT_CH, HID_CH))}
    _L1_gnn_all = _L1_gnn_setup()
    _L1_gnn_in = {k: v for k, v in _L1_gnn_all.items() if k in ('W1l', 'b1l', 'W1r', 'W2l', 'b2l', 'W2r')}
    del _L1_gnn_all
    return {'x': x, 'src': src, 'dst': dst, 'edge_weight': edge_weight, 'L0_gnn_Wm': _L0_gnn_in['Wm'], 'L0_gnn_bm': _L0_gnn_in['bm'], 'L0_gnn_W1': _L0_gnn_in['W1'], 'L0_gnn_b1': _L0_gnn_in['b1'], 'L0_gnn_W2': _L0_gnn_in['W2'], 'L0_gnn_b2': _L0_gnn_in['b2'], 'L1_gnn_W1l': _L1_gnn_in['W1l'], 'L1_gnn_b1l': _L1_gnn_in['b1l'], 'L1_gnn_W1r': _L1_gnn_in['W1r'], 'L1_gnn_W2l': _L1_gnn_in['W2l'], 'L1_gnn_b2l': _L1_gnn_in['b2l'], 'L1_gnn_W2r': _L1_gnn_in['W2r']}

def reference(x, src, dst, edge_weight, L0_gnn_Wm, L0_gnn_bm, L0_gnn_W1, L0_gnn_b1, L0_gnn_W2, L0_gnn_b2, L1_gnn_W1l, L1_gnn_b1l, L1_gnn_W1r, L1_gnn_W2l, L1_gnn_b2l, L1_gnn_W2r):
    import jax
    import jax.numpy as jnp

    def _L0_gnn_ref(z, edge_weight, edge_src, edge_dst, Wm, bm, W1, b1, W2, b2):
        import jax, jax.numpy as jnp
        import numpy as np
        N_NODES = 50000
        N_EDGES = 25000
        HID = 128
        n, H = z.shape
        Wd, Ws, ww = (Wm[:H], Wm[H:2 * H], Wm[2 * H])
        msgs = z[edge_dst] @ Wd + z[edge_src] @ Ws + edge_weight[:, None] * ww[None, :] + bm
        agg = jax.ops.segment_max(msgs, edge_dst, num_segments=n)
        deg = jax.ops.segment_sum(jnp.ones_like(edge_weight), edge_dst, num_segments=n)
        agg = jnp.where(deg[:, None] > 0, agg, jnp.zeros((), dtype=z.dtype))
        W1a, W1b = (W1[:H], W1[H:])
        hidden = jax.nn.relu(z @ W1a + agg @ W1b + b1)
        return hidden @ W2 + b2

    def _L1_gnn_ref(x, edge_index, W1l, b1l, W1r, W2l, b2l, W2r):
        import jax, jax.numpy as jnp
        import numpy as np
        N_NODES = 50000
        N_EDGES = 25000
        IN_CH, HID_CH, OUT_CH = (128, 256, 128)

        def _glorot(key, shape):
            fan_in, fan_out = (shape[1], shape[0])
            lim = float(np.sqrt(6.0 / (fan_in + fan_out)))
            return jax.random.uniform(key, shape, jnp.float32, -lim, lim)

        def _sage_conv(x, src, dst, Wl, bl, Wr, n_nodes):
            msg = x[src]
            agg = jax.ops.segment_sum(msg, dst, num_segments=n_nodes)
            deg = jax.ops.segment_sum(jnp.ones((src.shape[0],), x.dtype), dst, num_segments=n_nodes)
            mean = agg / jnp.maximum(deg, 1.0)[:, None]
            return mean @ Wl.T + bl + x @ Wr.T
        src, dst = (edge_index[0], edge_index[1])
        n = x.shape[0]
        h = _sage_conv(x, src, dst, W1l, b1l, W1r, n)
        h = jax.nn.relu(h)
        out = _sage_conv(h, src, dst, W2l, b2l, W2r, n)
        return out
    edge_index = jnp.stack([src, dst])
    x = _layernorm(x + _L0_gnn_ref(x, edge_weight, src, dst, L0_gnn_Wm, L0_gnn_bm, L0_gnn_W1, L0_gnn_b1, L0_gnn_W2, L0_gnn_b2), axis=-1)
    x = _layernorm(x + _L1_gnn_ref(x, edge_index, L1_gnn_W1l, L1_gnn_b1l, L1_gnn_W1r, L1_gnn_W2l, L1_gnn_b2l, L1_gnn_W2r), axis=-1)
    return x

_drawn_inputs = setup_inputs


def setup_inputs(seed=0):
    import zlib

    import numpy as np

    out = dict(_drawn_inputs(seed))
    spreads = {'L1_gnn_b1l': (0.0, 0.1), 'L1_gnn_b2l': (0.0, 0.1)}
    factors = {'edge_weight': 8.0}
    for name, (base, spread) in spreads.items():
        noise = np.random.default_rng([zlib.crc32(name.encode()), seed]).standard_normal(out[name].shape)
        drawn = base * np.exp(spread * noise) if base else spread * noise
        out[name] = jnp.asarray(drawn.astype(out[name].dtype))
    for name, factor in factors.items():
        out[name] = (out[name] * factor).astype(out[name].dtype)
    return out
```

```python
import concourse.bass as bass
from concourse import mybir
from contextlib import ExitStack

P = 128
N = 3125
F = 128
HID2 = 256
E = 100000
NT = -(-N // P)
LASTN = N - (NT - 1) * P
BS = 7
NB = 4
RING = NB * BS
ROUNDS = -(-E // (P * RING))
CHUNK = ROUNDS * RING
FULL = E // CHUNK
TAIL = E - FULL * CHUNK
NODST = 4095.0
BIG = 1.7e38
ROWS = P * CHUNK
GROUPS = [(t, min(4, NT - t)) for t in range(0, NT, 4)]
NG = len(GROUPS)
GB = 4
EPS = 1e-5


def skewed(stages):
    for s in range(NG + max(o for o, _ in stages)):
        for off, stage in sorted(stages, key=lambda x: -x[0]):
            if 0 <= s - off < NG:
                stage(s - off)


def gnn_kernel(nc, x, src, dst, w, Wm, bm, W1, b1, W2, b2, W1lT, b1l, W1rT, W2lT, b2l, W2rT, out):
    f32, i32 = mybir.dt.float32, mybir.dt.int32
    ALU, ACT = mybir.AluOpType, mybir.ActivationFunctionType

    def dram(name, shape, dt=f32):
        return nc.dram_tensor(name, shape, dt, kind="Internal").ap()

    zs_d = dram("zs_d", [NT * P, F])
    x1_d = dram("x1_d", [NT * P, F])
    g_d = dram("g_d", [NT * P, F])
    r_d = dram("r_d", [NT * P, F])
    xT_d = dram("xT_d", [P, NT * P])
    x1T_d = dram("x1T_d", [P, NT * P])
    dst_d = dram("dst_d", [P, CHUNK])
    run_d = [dram(f"run_d{q}", [ROWS + P, F]) for q in range(3)]

    ctx = ExitStack()
    with ctx:
        def sb(name, shape, dt=f32):
            return ctx.enter_context(nc.sbuf_tensor(name, shape, dt))

        def sem(name):
            return ctx.enter_context(nc.semaphore(name))

        src_i = sb("src_i", [P, CHUNK], i32)
        dst_i = sb("dst_i", [P, CHUNK], i32)
        dst_f = sb("dst_f", [P, CHUNK])
        w_s = sb("w_s", [P, CHUNK])
        same = sb("same", [P, CHUNK])
        keep = sb("keep", [P, CHUNK])
        gath = sb("gath", [P, RING, F])
        runs = sb("runs", [P, RING, F])
        idx = sb("idx", [P, RING], i32)
        ident = sb("ident", [P, P])
        shift = sb("shift", [P, P])
        wrap = sb("wrap", [P, P])
        ones = sb("ones", [P, P])
        zero = sb("zero", [P, P])
        eps = sb("eps", [P, 1])
        node_i = sb("node_i", [P, NT], i32)
        node = sb("node", [P, NT])
        diag = sb("diag", [P, 2, P])
        ends = sb("ends", [P, 2, P])
        cont = sb("cont", [P, P])
        whole = sb("whole", [P, P])
        ma = sb("ma", [P, 2, P])
        mb = sb("mb", [P, 2, P])
        junk = sb("junk", [P, CHUNK])
        above = sb("above", [P, NT])
        above_i = sb("above_i", [P, NT], i32)
        cnt = sb("cnt", [P, NT])
        end = sb("end", [P, NT])
        begin = sb("begin", [P, NT])
        pend = sb("pend", [P, NT])
        tmp = sb("tmp", [P, 4, NT])
        has = sb("has", [P, NT])
        scale = sb("scale", [P, NT])
        idx_end = sb("idx_end", [P, NT], i32)
        idx_car = sb("idx_car", [P, NT], i32)
        carry = sb("carry", [P, 2, P])
        carry_n = sb("carry_n", [P, F])
        wm = sb("wm", [P, 2, F])
        ww = sb("ww", [P, F])
        rows = sb("rows", [1, 3, F])
        w1 = sb("w1", [P, 2, F])
        w2 = sb("w2", [P, F])
        cols = sb("cols", [P, 3])
        w1l = sb("w1l", [P, HID2])
        w1r = sb("w1r", [P, HID2])
        w2l = sb("w2l", [P, 2, F])
        w2r = sb("w2r", [P, 2, F])
        tT = sb("tT", [P, GB, 512])
        tN = sb("tN", [P, GB, 4, F])
        agg = sb("agg", [P, 2, 4, F])
        aggT = sb("aggT", [P, 2, 512])
        hidT = sb("hidT", [P, 2, 2, 512])
        yv = sb("yv", [P, 2, 4, F])
        yo = sb("yo", [P, 2, 4, F])
        yT = sb("yT", [P, 2, 512])
        st = sb("st", [P, 2, 4, 6])
        mv = sb("mv", [P, 2, 4, 2])
        sd = sb("sd", [P, 2, 4])
        rs = sb("rs", [P, 2, 4])
        bank = [ctx.enter_context(nc.psum_tensor(f"bank{i}", [P, 512], f32)) for i in range(8)]

        clean = sem("clean")
        l_src, l_dst, l_w, l_x, l_par = (sem(n) for n in ("l_src", "l_dst", "l_w", "l_x", "l_par"))
        consts = sem("consts")
        order = sem("order")
        dst_ready, dst_stored = sem("dst_ready"), sem("dst_stored")
        diag_ready, ends_ps, above_ready = sem("diag_ready"), sem("ends_ps"), sem("above_ready")
        chunk_in = [sem(f"chunk_in{i}") for i in range(4)]
        chunk_used = sem("chunk_used")
        end_ready, begin_ps, idx_ready, masks_ready = sem("end_ready"), sem("begin_ps"), sem("idx_ready"), sem("masks_ready")
        x_T, x_Ts, zs_ps, zs_sb = sem("x_T"), sem("x_Ts"), sem("zs_ps"), sem("zs_sb")
        xT_st = [sem(f"xT_st{i}") for i in range(2)]
        zs_st = [sem(f"zs_st{i}") for i in range(2)]
        filled = [sem(f"filled{q}") for q in range(3)]
        stepped = [sem(f"stepped{q}") for q in range(3)]
        landed = [[sem(f"landed{q}_{b}") for b in range(NB)] for q in range(3)]
        dumped = [[sem(f"dumped{q}_{b}") for b in range(NB)] for q in range(3)]
        last_T = [sem(f"last_T{q}") for q in range(3)]
        car_sc = [sem(f"car_sc{q}") for q in range(3)]
        car_T = [sem(f"car_T{q}") for q in range(3)]
        car_sb = [sem(f"car_sb{q}") for q in range(3)]
        car_st = [sem(f"car_st{q}") for q in range(3)]
        res_in = [sem(f"res_in_{g}") for g in range(NG)]
        grp_in = [[sem(f"grp_in{q}_{i}") for i in range(GB)] for q in range(3)]
        zd_ps = sem("zd_ps")
        noted = sem("noted")
        agg_sb = [sem(f"agg_sb{q}") for q in range(3)]
        agg_T = [sem(f"agg_T{q}") for q in range(2)]
        agg_Ts = [sem(f"agg_Ts{q}") for q in range(2)]
        hid_ps = [sem(f"hid_ps{q}") for q in range(2)]
        hid_sb = [sem(f"hid_sb{q}") for q in range(2)]
        o_ps = [sem(f"o_ps{q}") for q in range(2)]
        var_sb = [sem(f"var_sb{q}") for q in range(3)]
        sd_sb = [sem(f"sd_sb{q}") for q in range(3)]
        y_sb = [sem(f"y_sb{q}") for q in range(3)]
        y_st = [[sem(f"y_st{q}_{i}") for i in range(2)] for q in range(3)]
        y_T, y_Ts = sem("y_T"), sem("y_Ts")
        yT_st = [sem(f"yT_st{i}") for i in range(2)]

        block = ctx.enter_context(nc.Block())

        def tiled(table, t, m):
            return table[t * P:(t + m) * P, :].rearrange("(t p) f -> p t f", p=P)

        def run_rows(q):
            return run_d[q][0:ROWS, :].rearrange("(p k) f -> p k f", k=CHUNK)

        runs_flat = runs[:, :, :].rearrange("p k f -> p (k f)")

        def chunk_buf(t):
            return runs_flat[:, (t % 4) * CHUNK:(t % 4 + 1) * CHUNK]

        @block.sync
        def _(sp):
            sp.wait_ge(clean, 4)
            for tile, table, s in ((dst_i, dst, l_dst), (src_i, src, l_src), (w_s, w, l_w)):
                sp.dma_start(tile[0:FULL, :], table[0:FULL * CHUNK].rearrange("(p k) -> p k", k=CHUNK)).then_inc(s, 16)
                sp.dma_start(tile[FULL:FULL + 1, 0:TAIL], table[FULL * CHUNK:E].rearrange("(p k) -> p k", p=1)).then_inc(s, 16)
            sp.dma_start(gath[:, 0:NT - 1, :], x[0:(NT - 1) * P, :].rearrange("(t p) f -> p t f", p=P)).then_inc(l_x, 16)
            sp.dma_start(gath[0:LASTN, NT - 1, :], x[(NT - 1) * P:N, :]).then_inc(l_x, 16)
            sp.wait_ge(dst_ready, 1)
            sp.dma_start(dst_d[:, :], dst_f[:, :]).then_inc(dst_stored, 16)
            for g, (t, m) in enumerate(GROUPS):
                sp.wait_ge(x_Ts, g + 1)
                sp.dma_start(xT_d[:, t * P:(t + m) * P], tT[:, g % 2, 0:m * P]).then_inc(xT_st[g % 2], 16)
                sp.wait_ge(zs_sb, g + 1)
                sp.dma_start(tiled(zs_d, t, m), yo[:, g % 2, 0:m, :]).then_inc(zs_st[g % 2], 16)

            def gather_pass(q):
                def turn(i):
                    for b in range(NB):
                        sp.wait_ge(stepped[q], i * RING + (b + 1) * BS)
                        sp.dma_start(run_rows(q)[:, bass.ds(i * RING + b * BS, BS), :],
                                     runs[:, b * BS:(b + 1) * BS, :]).then_inc(dumped[q][b], 16)
                with sp.Fori(0, ROUNDS) as i:
                    turn(i)
                sp.wait_ge(car_sb[q], 1)
                sp.dma_start(run_d[q][ROWS:ROWS + P, :], carry_n[:, :]).then_inc(car_st[q], 16)

            def load_group(q, tableT, table):
                def stage(g):
                    t, m = GROUPS[g]
                    if g >= GB:
                        sp.wait_ge(hid_ps[q], g - GB + 1)
                        sp.wait_ge(var_sb[q], g - GB + 1)
                    sp.dma_start(tT[:, g % GB, 0:m * P], tableT[:, t * P:(t + m) * P]).then_inc(grp_in[q][g % GB], 16)
                    if q == 0 and m + t == NT:
                        sp.dma_start(tN[0:LASTN, g % GB, 0, :], x[t * P:N, :]).then_inc(grp_in[q][g % GB], 16)
                    else:
                        sp.dma_start(tN[:, g % GB, 0:m, :], tiled(table, t, m)).then_inc(grp_in[q][g % GB], 16)
                return stage

            gather_pass(0)
            for i in range(2):
                sp.wait_ge(xT_st[i], 16 * len(range(i, NG, 2)))
                sp.wait_ge(zs_st[i], 16 * len(range(i, NG, 2)))

            def store_x1(g):
                t, m = GROUPS[g]
                sp.wait_ge(y_sb[0], g + 1)
                sp.dma_start(tiled(x1_d, t, m), yo[:, g % 2, 0:m, :]).then_inc(y_st[0][g % 2], 16)

            def store_x1T(g):
                t, m = GROUPS[g]
                sp.wait_ge(y_Ts, g + 1)
                sp.dma_start(x1T_d[:, t * P:(t + m) * P], yT[:, g % 2, 0:m * P]).then_inc(yT_st[g % 2], 16)

            skewed([(0, load_group(0, xT_d, x)), (4, store_x1), (5, store_x1T)])

            gather_pass(1)
            for i in range(2):
                sp.wait_ge(y_st[0][i], 16 * len(range(i, NG, 2)))
                sp.wait_ge(yT_st[i], 16 * len(range(i, NG, 2)))

            def store_gr(g):
                t, m = GROUPS[g]
                sp.wait_ge(y_sb[1], g + 1)
                sp.dma_start(tiled(g_d, t, m), yo[:, g % 2, 0:m, :]).then_inc(y_st[1][g % 2], 16)
                sp.dma_start(tiled(r_d, t, m), yv[:, g % 2, 0:m, :]).then_inc(y_st[1][g % 2], 16)

            skewed([(0, load_group(1, x1T_d, x1_d)), (4, store_gr)])

            gather_pass(2)
            for i in range(2):
                sp.wait_ge(y_st[1][i], 32 * len(range(i, NG, 2)))

            def load_r(g):
                t, m = GROUPS[g]
                if g >= GB:
                    sp.wait_ge(var_sb[2], g - GB + 1)
                sp.dma_start(tN[:, g % GB, 0:m, :], tiled(r_d, t, m)).then_inc(grp_in[2][g % GB], 16)

            def store_out(g):
                t, m = GROUPS[g]
                sp.wait_ge(y_sb[2], g + 1)
                if t + m < NT:
                    sp.dma_start(tiled(out, t, m), yo[:, g % 2, 0:m, :]).then_inc(y_st[2][g % 2], 16)
                else:
                    sp.dma_start(out[t * P:N, :], yo[0:LASTN, g % 2, 0, :]).then_inc(y_st[2][g % 2], 16)

            skewed([(0, load_r), (2, store_out)])
            for i in range(2):
                sp.wait_ge(y_st[2][i], 16 * len(range(i, NG, 2)))

        @block.scalar
        def _(act):
            for tile, table in (
                (wm[:, :, :], Wm[0:2 * F, :].rearrange("(a p) f -> p a f", p=P)),
                (ww[:, :], Wm[2 * F:2 * F + 1, :].broadcast_to([P, F])),
                (rows[0:1, 0, :], bm.rearrange("(a f) -> a f", a=1)),
                (rows[0:1, 1, :], b2.rearrange("(a f) -> a f", a=1)),
                (rows[0:1, 2, :], b2l.rearrange("(a f) -> a f", a=1)),
                (w1[:, :, :], W1.rearrange("(a p) f -> p a f", p=P)),
                (w2[:, :], W2),
                (cols[:, 0:1], b1.rearrange("(p a) -> p a", a=1)),
                (cols[:, 1:2], b1l[0:P].rearrange("(p a) -> p a", a=1)),
                (cols[:, 2:3], b1l[P:2 * P].rearrange("(p a) -> p a", a=1)),
                (w1l[:, :], W1lT), (w1r[:, :], W1rT),
                (w2l[:, :, :], W2lT.rearrange("(a p) f -> p a f", p=P)),
                (w2r[:, :, :], W2rT.rearrange("(a p) f -> p a f", p=P)),
            ):
                act.dma_start(tile, table).then_inc(l_par, 16)
            for g, (t, m) in enumerate(GROUPS):
                act.wait_ge(x_T, g + 1)
                if g >= 2:
                    act.wait_ge(zs_ps, g - 1)
                    act.wait_ge(xT_st[g % 2], 16 * (g // 2))
                nc.scalar.copy(tT[:, g % 2, 0:m * P], bank[g % 2][:, 0:m * P]).then_inc(x_Ts, 1)

            def gather_pass(q):
                def turn(i, first):
                    for b in range(NB):
                        if not first:
                            act.wait_ge(stepped[q], (i - 1) * RING + (b + 1) * BS)
                        last = nc.scalar.copy(idx[:, b * BS:(b + 1) * BS], src_i[:, bass.ds(i * RING + b * BS, BS)])
                        if q == 0:
                            for j in range(BS):
                                last = nc.scalar.activation(gath[:, b * BS + j, :], ww[:, :], ACT.Copy,
                                                            scale=w_s[:, bass.ds(i * RING + b * BS + j, 1)])
                        last.then_inc(filled[q], 1)
                turn(0, True)
                with act.Fori(1, ROUNDS) as i:
                    turn(i, False)

            def root(q):
                def stage(g):
                    m = GROUPS[g][1]
                    act.wait_ge(var_sb[q], g + 1)
                    if g >= 2:
                        act.wait_ge(y_sb[q], g - 1)
                    nc.scalar.activation(sd[:, g % 2, 0:m], mv[:, g % 2, 0:m, 1], ACT.Sqrt,
                                         bias=eps[:, :]).then_inc(sd_sb[q], 1)
                return stage

            def copy_aggT(q):
                def stage(g):
                    m = GROUPS[g][1]
                    act.wait_ge(agg_T[q], g + 1)
                    if g >= 2:
                        act.wait_ge(hid_ps[q], g - 1)
                    nc.scalar.copy(aggT[:, g % 2, 0:m * P], bank[2][:, 0:m * P]).then_inc(agg_Ts[q], 1)
                return stage

            def relu(q, halves):
                def stage(g):
                    m = GROUPS[g][1]
                    act.wait_ge(hid_ps[q], g + 1)
                    if g >= 2:
                        act.wait_ge(o_ps[q], g - 1)
                    for a in range(halves):
                        last = nc.scalar.activation(hidT[:, g % 2, a, 0:m * P], bank[3 + a][:, 0:m * P], ACT.Relu,
                                                    bias=cols[:, q + a:q + a + 1])
                    last.then_inc(hid_sb[q], 1)
                return stage

            def copy_x1T(g):
                m = GROUPS[g][1]
                act.wait_ge(y_T, g + 1)
                if g >= 2:
                    act.wait_ge(yT_st[g % 2], 16 * (g // 2))
                nc.scalar.copy(yT[:, g % 2, 0:m * P], bank[7][:, 0:m * P]).then_inc(y_Ts, 1)

            act.wait_ge(l_par, 16 * 14)
            act.wait_ge(l_src, 32)
            act.wait_ge(l_w, 32)
            gather_pass(0)
            skewed([(1, copy_aggT(0)), (2, relu(0, 1)), (3, root(0)), (5, copy_x1T)])
            gather_pass(1)
            skewed([(1, copy_aggT(1)), (2, relu(1, 2))])
            gather_pass(2)
            skewed([(1, root(2))])

        @block.gpsimd
        def _(pool):
            nc.gpsimd.iota(node_i[:, :], pattern=[[P, NT]], base=0, channel_multiplier=1).then_inc(consts, 1)
            pool.wait_ge(clean, 5)
            nc.gpsimd.affine_select(out=ident[:, :], in_=ident[:, :], compare_op=ALU.not_equal, fill=1.0, base=0,
                                    pattern=[[-1, P]], channel_multiplier=1).then_inc(consts, 1)
            nc.gpsimd.affine_select(out=shift[:, :], in_=shift[:, :], compare_op=ALU.not_equal, fill=1.0, base=1,
                                    pattern=[[-1, P]], channel_multiplier=1).then_inc(consts, 1)
            nc.gpsimd.affine_select(out=wrap[:, :], in_=wrap[:, :], compare_op=ALU.not_equal, fill=1.0, base=P - 1,
                                    pattern=[[1, P]], channel_multiplier=-1).then_inc(consts, 1)
            pool.wait_ge(above_ready, 1)
            pool.wait_ge(dst_stored, 16)
            for t in range(NT):
                if t >= 4:
                    pool.wait_ge(chunk_used, t - 3)
                pool.indirect_dma_start(chunk_buf(t), None, dst_d[:, :],
                                        bass.IndirectOffsetOnAxis(ap=above_i[:, t:t + 1], axis=0)).then_inc(chunk_in[t % 4], 16)

            def gather_pass(q, table):
                def turn(i):
                    for b in range(NB):
                        pool.wait_ge(filled[q], i * NB + b + 1)
                        pool.sem_inc(noted, 1)
                        for j in range(b * BS, (b + 1) * BS):
                            pool.indirect_dma_start(gath[:, j, :], None, table,
                                                    bass.IndirectOffsetOnAxis(ap=idx[:, j:j + 1], axis=0),
                                                    compute_op=ALU.add if q == 0 else ALU.bypass).then_inc(landed[q][b], 16)
                with pool.Fori(0, ROUNDS) as i:
                    turn(i)
                for b in range(NB):
                    pool.wait_ge(dumped[q][b], 16 * ROUNDS)
                pool.wait_ge(idx_ready, 1)
                pool.wait_ge(stepped[q], CHUNK)
                pool.wait_ge(car_st[q], 16)
                for g, (t0, m) in enumerate(GROUPS):
                    for t in range(t0, t0 + m):
                        pool.indirect_dma_start(gath[:, t, :], None, run_d[q][:, :],
                                                bass.IndirectOffsetOnAxis(ap=idx_end[:, t:t + 1], axis=0)).then_inc(res_in[g], 16)
                        pool.indirect_dma_start(runs[:, t, :], None, run_d[q][:, :],
                                                bass.IndirectOffsetOnAxis(ap=idx_car[:, t:t + 1], axis=0)).then_inc(res_in[g], 16)

            for i in range(2):
                pool.wait_ge(zs_st[i], 16 * len(range(i, NG, 2)))
            gather_pass(0, zs_d[:, :])
            for i in range(2):
                pool.wait_ge(y_st[0][i], 16 * len(range(i, NG, 2)))
            gather_pass(1, x1_d[:, :])
            for i in range(2):
                pool.wait_ge(y_st[1][i], 32 * len(range(i, NG, 2)))
            gather_pass(2, g_d[:, :])

        @block.vector
        def _(dve):
            made = [0]

            def link(ins):
                made[0] += 1
                ins.then_inc(order, 1)
                dve.wait_ge(order, made[0])

            nc.vector.memset(dst_i[:, :], int(NODST)).then_inc(clean, 1)
            nc.vector.memset(src_i[:, :], 0).then_inc(clean, 1)
            nc.vector.memset(w_s[:, :], 0.0).then_inc(clean, 1)
            nc.vector.memset(gath[:, NT - 1, :], 0.0).then_inc(clean, 1)
            nc.vector.memset(ident[:, :], 0.0)
            nc.vector.memset(shift[:, :], 0.0)
            nc.vector.memset(wrap[:, :], 0.0).then_inc(clean, 1)
            nc.vector.memset(ones[:, :], 1.0)
            nc.vector.memset(zero[:, :], 0.0)
            nc.vector.memset(tN[:, :, :, :], 0.0)
            nc.vector.memset(same[:, 0:1], 0.0)
            nc.vector.memset(cont[:, 0:1], 0.0)
            nc.vector.memset(whole[:, 0:1], 0.0)
            link(nc.vector.memset(eps[:, :], EPS))

            dve.wait_ge(l_dst, 32)
            nc.vector.tensor_copy(dst_f[:, :], dst_i[:, :]).then_inc(dst_ready, 1)
            dve.wait_ge(dst_ready, 1)
            dve.wait_ge(consts, 4)
            nc.vector.tensor_scalar(diag[:, 0, :], ident[:, :], dst_f[:, 0:1], None, ALU.mult)
            nc.vector.tensor_scalar(diag[:, 1, :], ident[:, :], dst_f[:, CHUNK - 1:CHUNK], None, ALU.mult).then_inc(diag_ready, 1)
            nc.vector.tensor_copy(node[:, :], node_i[:, :])
            link(nc.vector.tensor_tensor(same[:, 1:CHUNK], dst_f[:, 1:CHUNK], dst_f[:, 0:CHUNK - 1], ALU.is_equal))
            link(nc.vector.tensor_scalar(keep[:, :], same[:, :], 2 * BIG, -BIG, ALU.mult, ALU.add))
            dve.wait_ge(ends_ps, 1)
            link(nc.vector.tensor_copy(ends[:, :, :], bank[4][:, 0:2 * P].rearrange("p (a c) -> p a c", a=2)))
            for t in range(NT):
                last = nc.vector.tensor_scalar(junk[:, 0:P], ends[:, 1, :], node[:, t:t + 1], None,
                                               ALU.is_le, ALU.add, accum_out=above[:, t:t + 1])
                link(last)
            nc.vector.tensor_copy(above_i[:, :], above[:, :]).then_inc(above_ready, 1)
            nc.vector.tensor_tensor(cont[:, 1:P], ends[:, 0, 1:P], ends[:, 1, 0:P - 1], ALU.is_equal)
            link(nc.vector.tensor_tensor(whole[:, 1:P], ends[:, 0, 0:P - 1], ends[:, 1, 0:P - 1], ALU.is_equal))
            nc.vector.tensor_copy(mb[:, 1, :], cont[:, :])
            link(nc.vector.tensor_tensor(ma[:, 1, :], cont[:, :], whole[:, :], ALU.mult))
            nc.vector.tensor_scalar(mb[:, 0, :], cont[:, :], 2 * BIG, -BIG, ALU.mult, ALU.add)
            link(nc.vector.tensor_scalar(ma[:, 0, :], ma[:, 1, :], 2 * BIG, -BIG, ALU.mult, ALU.add))

            for g, (t, m) in enumerate(GROUPS):
                dve.wait_ge(zs_ps, g + 1)
                if g >= 2:
                    dve.wait_ge(zs_st[g % 2], 16 * (g // 2))
                nc.vector.tensor_copy(yo[:, g % 2, 0:m, :],
                                      bank[2 + g % 2][:, 0:m * P].rearrange("p (t f) -> p t f", f=F)).then_inc(zs_sb, 1)

            for t in range(NT):
                dve.wait_ge(chunk_in[t % 4], 16 * (t // 4 + 1))
                nc.vector.tensor_scalar(junk[:, :], chunk_buf(t), node[:, t:t + 1], None, ALU.is_le, ALU.add,
                                        accum_out=cnt[:, t:t + 1]).then_inc(chunk_used, 1)
                dve.wait_ge(chunk_used, t + 1)
            nc.vector.tensor_scalar(tmp[:, 0, :], cnt[:, :], 0.0, None, ALU.is_equal)
            nc.vector.scalar_tensor_tensor(end[:, :], above[:, :], float(CHUNK), cnt[:, :], ALU.mult, ALU.add).then_inc(end_ready, 1)
            dve.wait_ge(end_ready, 1)
            nc.vector.tensor_scalar(tmp[:, 1, :], end[:, :], -1.0, 0.0, ALU.add, ALU.max)
            link(nc.vector.tensor_tensor(pend[:, :], above[:, :], tmp[:, 0, :], ALU.subtract))
            dve.wait_ge(begin_ps, 1)
            link(nc.vector.tensor_copy(begin[:, :], bank[4][:, 0:NT]))
            nc.vector.tensor_copy(idx_end[:, :], tmp[:, 1, :])
            link(nc.vector.tensor_tensor(tmp[:, 2, :], end[:, :], begin[:, :], ALU.subtract))
            nc.vector.tensor_scalar(has[:, :], tmp[:, 2, :], 0.0, None, ALU.is_gt)
            link(nc.vector.tensor_scalar(tmp[:, 3, :], tmp[:, 2, :], 1.0, None, ALU.max))
            link(nc.vector.reciprocal(tmp[:, 0, :], tmp[:, 3, :]))
            nc.vector.tensor_tensor(scale[:, :], tmp[:, 0, :], has[:, :], ALU.mult)
            link(nc.vector.scalar_tensor_tensor(tmp[:, 1, :], pend[:, :], float(CHUNK), begin[:, :], ALU.mult, ALU.is_gt))
            link(nc.vector.tensor_tensor(tmp[:, 2, :], tmp[:, 1, :], pend[:, :], ALU.mult))
            link(nc.vector.tensor_scalar(tmp[:, 3, :], tmp[:, 2, :], float(ROWS), None, ALU.add))
            nc.vector.tensor_copy(idx_car[:, :], tmp[:, 3, :]).then_inc(idx_ready, 1)

            def gather_pass(q):
                op0, op1 = (ALU.min, ALU.max) if q == 0 else (ALU.mult, ALU.add)
                mask = keep if q == 0 else same
                v = 0 if q == 0 else 1
                link(nc.vector.memset(runs[:, RING - 1, :], 0.0))

                def turn(i, first):
                    for b in range(NB):
                        dve.wait_ge(landed[q][b], 16 * BS * i + 16 * BS)
                        if not first:
                            dve.wait_ge(dumped[q][b], 16 * i)
                        for j in range(b * BS, (b + 1) * BS):
                            if not (first and j == 0):
                                dve.wait_ge(stepped[q], i * RING + j)
                            nc.vector.scalar_tensor_tensor(
                                runs[:, j, :], runs[:, (j - 1) % RING, :], mask[:, bass.ds(i * RING + j, 1)],
                                gath[:, j, :], op0, op1).then_inc(stepped[q], 1)
                turn(0, True)
                with dve.Fori(1, ROUNDS) as i:
                    turn(i, False)
                dve.wait_ge(last_T[q], 1)
                nc.vector.memset(carry[:, 0, 0:1], -BIG if q == 0 else 0.0)
                link(nc.vector.tensor_tensor(carry[:, 0, 1:P], bank[4][:, 0:P - 1], mb[:, v, 1:P], op0))
                nc.vector.tensor_tensor_scan(carry[:, 1, :], ma[:, v, :], carry[:, 0, :], 0.0, op0, op1).then_inc(car_sc[q], 1)
                dve.wait_ge(car_T[q], 1)
                nc.vector.tensor_copy(carry_n[:, :], bank[5][:, 0:F]).then_inc(car_sb[q], 1)

            def joined(q, g):
                dve.wait_ge(res_in[g], 32 * GROUPS[g][1] * (q + 1))

            def per_node(v, t, m):
                return v[:, t:t + m].unsqueeze(2).broadcast_to([P, m, F])

            def join0(g):
                t, m = GROUPS[g]
                joined(0, g)
                dve.wait_ge(zd_ps, g + 1)
                if g >= 2:
                    dve.wait_ge(agg_T[0], g - 1)
                a = agg[:, g % 2, 0:m, :]
                link(nc.vector.tensor_tensor(a, gath[:, t:t + m, :], runs[:, t:t + m, :], ALU.max))
                link(nc.vector.tensor_tensor(a, a, bank[g % 2][:, 0:m * P].rearrange("p (t f) -> p t f", f=F), ALU.add))
                nc.vector.tensor_tensor(a, a, per_node(has, t, m), ALU.mult).then_inc(agg_sb[0], 1)

            def stats(q, g):
                m = GROUPS[g][1]
                for j in range(m):
                    last = nc.vector.bn_stats(st[:, g % 2, j, :], yv[:, g % 2, j, :])
                link(last)
                for j in range(m):
                    last = nc.vector.bn_aggr(mv[:, g % 2, j, :], st[:, g % 2, j, :])
                last.then_inc(var_sb[q], 1)

            def residual0(g):
                m = GROUPS[g][1]
                dve.wait_ge(o_ps[0], g + 1)
                dve.wait_ge(grp_in[0][g % GB], 32 * (g // GB + 1))
                if g >= 2:
                    dve.wait_ge(y_sb[0], g - 1)
                link(nc.vector.tensor_tensor(yv[:, g % 2, 0:m, :], bank[5 + g % 2][:, 0:m * P].rearrange("p (t f) -> p t f", f=F),
                                             tN[:, g % GB, 0:m, :], ALU.add))
                stats(0, g)

            def norm(q):
                def stage(g):
                    m = GROUPS[g][1]
                    dve.wait_ge(sd_sb[q], g + 1)
                    if g >= 2:
                        dve.wait_ge(y_st[q][g % 2], 16 * (g // 2))
                        if q == 0:
                            dve.wait_ge(y_T, g - 1)
                    link(nc.vector.reciprocal(rs[:, g % 2, 0:m], sd[:, g % 2, 0:m]))
                    for j in range(m):
                        last = nc.vector.tensor_scalar(yo[:, g % 2, j, :], yv[:, g % 2, j, :], mv[:, g % 2, j, 0:1],
                                                       rs[:, g % 2, j:j + 1], ALU.subtract, ALU.mult)
                    last.then_inc(y_sb[q], 1)
                return stage

            def join1(g):
                t, m = GROUPS[g]
                joined(1, g)
                if g >= 2:
                    dve.wait_ge(agg_T[1], g - 1)
                a = agg[:, g % 2, 0:m, :]
                link(nc.vector.tensor_tensor(a, gath[:, t:t + m, :], runs[:, t:t + m, :], ALU.add))
                nc.vector.tensor_tensor(a, a, per_node(scale, t, m), ALU.mult).then_inc(agg_sb[1], 1)

            def take1(g):
                m = GROUPS[g][1]
                dve.wait_ge(o_ps[1], g + 1)
                dve.wait_ge(grp_in[1][g % GB], 32 * (g // GB + 1))
                if g >= 2:
                    dve.wait_ge(y_st[1][g % 2], 32 * (g // 2))
                nc.vector.tensor_copy(yo[:, g % 2, 0:m, :], bank[5][:, 0:m * P].rearrange("p (t f) -> p t f", f=F))
                nc.vector.tensor_tensor(yv[:, g % 2, 0:m, :], bank[6][:, 0:m * P].rearrange("p (t f) -> p t f", f=F),
                                        tN[:, g % GB, 0:m, :], ALU.add).then_inc(y_sb[1], 1)
                dve.wait_ge(y_sb[1], g + 1)
                nc.vector.memset(st[:, g % 2, 0, 0:1], 0.0).then_inc(var_sb[1], 1)

            def join2(g):
                t, m = GROUPS[g]
                joined(2, g)
                dve.wait_ge(grp_in[2][g % GB], 16 * (g // GB + 1))
                if g >= 2:
                    dve.wait_ge(y_sb[2], g - 1)
                link(nc.vector.tensor_tensor(agg[:, g % 2, 0:m, :], gath[:, t:t + m, :], runs[:, t:t + m, :], ALU.add))
                for j in range(m):
                    last = nc.vector.scalar_tensor_tensor(yv[:, g % 2, j, :], agg[:, g % 2, j, :], scale[:, t + j:t + j + 1],
                                                          tN[:, g % GB, j, :], ALU.mult, ALU.add)
                link(last)
                stats(2, g)

            gather_pass(0)
            skewed([(1, join0), (3, residual0), (4, norm(0))])
            gather_pass(1)
            skewed([(1, join1), (3, take1)])
            gather_pass(2)
            skewed([(1, join2), (2, norm(2))])

        @block.tensor
        def _(pe):
            pe.wait_ge(diag_ready, 1)
            for a in range(2):
                last = nc.tensor.matmul(bank[4][:, a * P:(a + 1) * P], ones[:, :], diag[:, a, :], start=True, stop=True)
            last.then_inc(ends_ps, 1)
            pe.wait_ge(l_x, 32)
            pe.wait_ge(l_par, 16 * 14)
            for g in range(NG + 1):
                if g < NG:
                    t, m = GROUPS[g]
                    if g >= 2:
                        pe.wait_ge(x_Ts, g - 1)
                    for j in range(m):
                        last = nc.tensor.transpose(bank[g % 2][:, j * P:(j + 1) * P], gath[:, t + j, :], ident[:, :])
                    last.then_inc(x_T, 1)
                if g:
                    h, (t, m) = g - 1, GROUPS[g - 1]
                    pe.wait_ge(x_Ts, h + 1)
                    if h >= 2:
                        pe.wait_ge(zs_sb, h - 1)
                    for j in range(m):
                        last = nc.tensor.matmul(bank[2 + h % 2][:, j * P:(j + 1) * P], tT[:, h % 2, j * P:(j + 1) * P],
                                                wm[:, 1, :], start=True, stop=True)
                    last.then_inc(zs_ps, 1)
            pe.wait_ge(end_ready, 1)
            nc.tensor.matmul(bank[4][:, 0:NT], shift[:, :], end[:, :], start=True, stop=False)
            nc.tensor.matmul(bank[4][:, 1:NT], wrap[:, :], end[:, 0:NT - 1], start=False, stop=True).then_inc(begin_ps, 1)

            def carries(q):
                pe.wait_ge(stepped[q], CHUNK)
                nc.tensor.transpose(bank[4][:, 0:P], runs[:, RING - 1, :], ident[:, :]).then_inc(last_T[q], 1)
                pe.wait_ge(car_sc[q], 1)
                nc.tensor.transpose(bank[5][:, 0:P], carry[:, 1, :], ident[:, :]).then_inc(car_T[q], 1)

            def product_zd(g):
                m = GROUPS[g][1]
                pe.wait_ge(grp_in[0][g % GB], 32 * (g // GB + 1))
                if g >= 2:
                    pe.wait_ge(agg_sb[0], g - 1)
                for j in range(m):
                    o = bank[g % 2][:, j * P:(j + 1) * P]
                    nc.tensor.matmul(o, tT[:, g % GB, j * P:(j + 1) * P], wm[:, 0, :], start=True, stop=False)
                    last = nc.tensor.matmul(o, ones[0:1, :], rows[0:1, 0, :], start=False, stop=True)
                last.then_inc(zd_ps, 1)

            def agg_transposed(q):
                def stage(g):
                    m = GROUPS[g][1]
                    pe.wait_ge(agg_sb[q], g + 1)
                    if g >= 1:
                        pe.wait_ge(agg_Ts[q], g)
                    for j in range(m):
                        last = nc.tensor.transpose(bank[2][:, j * P:(j + 1) * P], agg[:, g % 2, j, :], ident[:, :])
                    last.then_inc(agg_T[q], 1)
                return stage

            def hidden(q, wa, wb, halves):
                def stage(g):
                    m = GROUPS[g][1]
                    pe.wait_ge(agg_Ts[q], g + 1)
                    pe.wait_ge(grp_in[q][g % GB], 32 * (g // GB + 1))
                    if g >= 1:
                        pe.wait_ge(hid_sb[q], g)
                    for a in range(halves):
                        o = bank[3 + a][:, 0:m * P]
                        nc.tensor.matmul(o, wa[:, a * P:(a + 1) * P], tT[:, g % GB, 0:m * P], start=True, stop=False)
                        last = nc.tensor.matmul(o, wb[:, a * P:(a + 1) * P], aggT[:, g % 2, 0:m * P], start=False, stop=True)
                    last.then_inc(hid_ps[q], 1)
                return stage

            def out0(g):
                m = GROUPS[g][1]
                pe.wait_ge(hid_sb[0], g + 1)
                if g >= 2:
                    pe.wait_ge(var_sb[0], g - 1)
                for j in range(m):
                    o = bank[5 + g % 2][:, j * P:(j + 1) * P]
                    nc.tensor.matmul(o, hidT[:, g % 2, 0, j * P:(j + 1) * P], w2[:, :], start=True, stop=False)
                    last = nc.tensor.matmul(o, ones[0:1, :], rows[0:1, 1, :], start=False, stop=True)
                last.then_inc(o_ps[0], 1)

            def x1_transposed(g):
                m = GROUPS[g][1]
                pe.wait_ge(y_sb[0], g + 1)
                if g >= 1:
                    pe.wait_ge(y_Ts, g)
                for j in range(m):
                    last = nc.tensor.transpose(bank[7][:, j * P:(j + 1) * P], yo[:, g % 2, j, :], ident[:, :])
                last.then_inc(y_T, 1)

            def out1(g):
                m = GROUPS[g][1]
                pe.wait_ge(hid_sb[1], g + 1)
                if g >= 1:
                    pe.wait_ge(y_sb[1], g)
                for j in range(m):
                    for o, wt in ((bank[5][:, j * P:(j + 1) * P], w2l), (bank[6][:, j * P:(j + 1) * P], w2r)):
                        for a in range(2):
                            last = nc.tensor.matmul(o, hidT[:, g % 2, a, j * P:(j + 1) * P], wt[:, a, :],
                                                    start=a == 0, stop=a == 1 and wt is w2l)
                        if wt is w2r:
                            last = nc.tensor.matmul(o, ones[0:1, :], rows[0:1, 2, :], start=False, stop=True)
                last.then_inc(o_ps[1], 1)

            carries(0)
            w1f = w1[:, :, :].rearrange("p a f -> p (a f)")
            skewed([(0, product_zd), (1, agg_transposed(0)), (2, hidden(0, w1f[:, 0:F], w1f[:, F:2 * F], 1)),
                    (3, out0), (5, x1_transposed)])
            carries(1)
            skewed([(1, agg_transposed(1)), (2, hidden(1, w1r, w1l, 2)), (3, out1)])
            carries(2)


_INS = ["x", "src", "dst", "edge_weight", "L0_gnn_Wm", "L0_gnn_bm", "L0_gnn_W1", "L0_gnn_b1", "L0_gnn_W2", "L0_gnn_b2",
        "L1_gnn_W1l", "L1_gnn_b1l", "L1_gnn_W1r", "L1_gnn_W2l", "L1_gnn_b2l", "L1_gnn_W2r"]
_TRANSPOSED = ["L1_gnn_W1l", "L1_gnn_W1r", "L1_gnn_W2l", "L1_gnn_W2r"]


def kernel(**inputs):
    import numpy as np
    import concourse.bacc as bacc
    from concourse import mybir as _mybir
    from concourse.bass_utils import run_bass_kernel_spmd as run

    nc = bacc.Bacc("TRN2", target_bir_lowering=False, num_devices=1)
    arrays, args = {}, []
    for name in _INS:
        a = np.asarray(inputs[name])
        a = np.ascontiguousarray(a.T if name in _TRANSPOSED else a)
        arrays[f"in_{name}_dram"] = a
        args.append(nc.dram_tensor(f"in_{name}_dram", a.shape, _mybir.dt.from_np(a.dtype), kind="ExternalInput").ap())
    args.append(nc.dram_tensor("out_0_dram", (N, F), _mybir.dt.float32, kind="ExternalOutput").ap())
    gnn_kernel(nc, *args)
    r = run(nc, [arrays], core_ids=[0])
    return r.results[0]["out_0_dram"]
```

```python
import concourse.bass as bass
from concourse import mybir
from contextlib import ExitStack

P = 128
N = 3125
F = 128
HID2 = 256
E = 100000
NT = -(-N // P)
LASTN = N - (NT - 1) * P
BS = 4
NB = 4
RING = NB * BS
ROUNDS = -(-E // (P * RING))
CHUNK = ROUNDS * RING
FULL = E // CHUNK
TAIL = E - FULL * CHUNK
NODST = 4095.0
BIG = 1.7e38
ROWS = P * CHUNK
GT = 2
GROUPS = [(t, min(GT, NT - t)) for t in range(0, NT, GT)]
NG = len(GROUPS)
GB = 4
EPS = 1e-5
RG = RING // GT
SUB = 2
BATCH = SUB * P
NBATCH = -(-E // BATCH)
BB = -(-NBATCH // P)
BLAST = NBATCH - (BB - 1) * P
WIN = 10
COLS = WIN * NT
NWIN = -(-N // WIN)
WB = -(-NWIN // P)
RP = 15
PR = 5
LAG = 3
OFFS = 15
WINDOWS = ("COLS times a pair's window, which is the number of NWIN ordered window starts at or before the pair, less "
           "one; the first of them is pair 0")
PROUNDS = -(-(NBATCH + NWIN - 1) // RP)
PAIRS = PROUNDS * RP
HALF = -(-PAIRS // 2)
LEAD = 2
LASTM = 64
ADJ = ((NT - 1) * P + LASTM) * NT
ADJ_BANKS = (0, 1, 7)
ZW = 392
ZPIECE = 5 * ZW
ZROUNDS = 16
SETUP = ZROUNDS * ZPIECE
SAFE = (ADJ // 2 - SETUP) * 2 // COLS // RP
DENSE_MAX = 255
BY_ACT = (0, 1, 2, 4, 5, 6, 8, 9, 10, 12, 13, 14)


def skewed(stages):
    for s in range(NG + max(o for o, _ in stages)):
        for off, stage in sorted(stages, key=lambda x: -x[0]):
            if 0 <= s - off < NG:
                stage(s - off)


def gnn_kernel(nc, x, src, dst, w, Wm, bm, W1, b1, W2, b2, W1lT, b1l, W1rT, W2lT, b2l, W2rT, out):
    f32, i32, bf16 = mybir.dt.float32, mybir.dt.int32, mybir.dt.bfloat16
    ALU, ACT = mybir.AluOpType, mybir.ActivationFunctionType

    def dram(name, shape, dt=f32):
        return nc.dram_tensor(name, shape, dt, kind="Internal").ap()

    zs_d = dram("zs_d", [NT * P, F])
    x1_d = dram("x1_d", [NT * P, F])
    g_d = dram("g_d", [NT * P, F])
    r_d = dram("r_d", [NT * P, F])
    xT_d = dram("xT_d", [P, NT * P])
    x1T_d = dram("x1T_d", [P, NT * P])
    dst_d = dram("dst_d", [P, CHUNK])
    run_d = [dram(f"run_d{q}", [ROWS, F]) for q in range(3)]

    ctx = ExitStack()
    with ctx:
        def sb(name, shape, dt=f32):
            return ctx.enter_context(nc.sbuf_tensor(name, shape, dt))

        def sem(name):
            return ctx.enter_context(nc.semaphore(name))

        def carve(base, *shapes):
            at, views = 0, []
            for dt, *dims in shapes:
                words = 1
                for d in dims:
                    words *= d
                words = words // 2 if dt == bf16 else words
                v = base[:, at:at + words]
                v = v if dt == f32 else v.bitcast(dt)
                if len(dims) == 2:
                    v = v.rearrange("p (a b) -> p a b", b=dims[1])
                if len(dims) == 3:
                    v = v.rearrange("p (a b c) -> p a b c", b=dims[1], c=dims[2])
                at += words
                views.append(v)
            assert at <= base.shape[1], (at, base.shape)
            return views

        src_i = sb("src_i", [P, CHUNK], i32)
        keep = sb("keep", [P, CHUNK])
        idx = sb("idx", [P, RING], i32)
        ident = sb("ident", [P, P])
        ones = sb("ones", [P, P])
        eps = sb("eps", [P, 1])
        ma = sb("ma", [P, 2, P])
        mb = sb("mb", [P, 2, P])
        has = sb("has", [P, NT])
        scale = sb("scale", [P, NT])
        idx_end = sb("idx_end", [P, NT], i32)
        idx_fix = sb("idx_fix", [P, 1], i32)
        fix = sb("fix", [P, F])
        zeros = sb("zeros", [P, ZW])
        large = sb("large", [P, 1], i32)
        carry = sb("carry", [P, 2, P])
        ww = sb("ww", [P, F])
        rows = sb("rows", [1, 3, F])
        cols = sb("cols", [P, 3])
        st = sb("st", [P, 2, GT, 6])
        mv = sb("mv", [P, 2, GT, 2])
        sd = sb("sd", [P, 2, GT])
        rs = sb("rs", [P, 2, GT])

        adj_w = sb("adj_w", [P, ADJ // 2])
        adj = adj_w[:, :].bitcast(bf16)
        adj_v = adj.rearrange("p (n h) -> p n h", h=NT)
        (xin, chunks, dst_i, dst_f, same, junk, es_i, ed_i, eh_i, el_i, ed_f, eh_f, el_f, ek, hot, below, from_pos,
         pair_i, pair, win, batch, wstart_i, wstart, numbers_i, numbers, diag, ends, cont, whole, shift, wrap,
         xT_s, zs_s, ws, node_i, node, above, above_i, cnt, end, begin, tmp, pos, over) = carve(
            adj_w[:, ADJ // 2 - SETUP:],
            (f32, NT, F),
            (f32, 4, CHUNK),
            (i32, CHUNK), (f32, CHUNK), (f32, CHUNK),
            (f32, CHUNK),
            (i32, BB, BATCH), (i32, BB, BATCH),
            (i32, BB, BATCH), (i32, BB, BATCH),
            (f32, BB, BATCH), (f32, BB, BATCH), (f32, BB, BATCH),
            (f32, BB, BATCH),
            (f32, BB, PAIRS),
            (f32, BB, WB * P),
            (f32, WB, PAIRS),
            (i32, PAIRS), (f32, PAIRS), (f32, PAIRS), (f32, PAIRS),
            (i32, WB * P), (f32, WB * P),
            (i32, BB), (f32, BB),
            (f32, 2, P), (f32, 2, P),
            (f32, P),
            (f32, P),
            (f32, P), (f32, P),
            (f32, 4, GT * P), (f32, 4, GT * P),
            (f32, F),
            (i32, NT), (f32, NT),
            (f32, NT), (i32, NT),
            (f32, NT), (f32, NT), (f32, NT),
            (f32, 4, NT), (f32, WB), (f32, 2))

        rings = sb("rings", [P, max(2 * RING * F, NT * 3 * F // 2)])
        gath, runs = carve(rings, (f32, RING, F), (f32, RING, F))
        parts, = carve(rings, (bf16, NT, 3 * F))

        late = sb("late", [P, CHUNK + 4 * PAIRS + PAIRS + LAG + PR * SUB * (COLS + P) // 2 + 3 * P + COLS // 2 + P])
        w_s, key, nlo, off, hot_d, hot_l, sq, iota_d, iota_l, niota_l = carve(
            late, (f32, CHUNK),
            (f32, SUB, PAIRS),
            (f32, SUB, PAIRS),
            (i32, PAIRS + LAG),
            (bf16, PR, SUB * COLS), (bf16, PR, SUB * P), (bf16, 2, BATCH),
            (bf16, COLS), (bf16, P), (bf16, P))
        tT, tN, agg, aggT, hidT, yv, yo, w1l, w1r, w2l, w2r, w1, w2, wd = carve(
            late, (f32, GB, GT * P),
            (f32, GB, GT * P),
            (f32, 2, GT * P), (f32, 2, GT * P), (f32, 2, 2 * GT * P), (f32, 2, GT * P), (f32, 2, GT * P),
            (f32, HID2), (f32, HID2), (f32, 2, F), (f32, 2, F), (f32, 2, F), (f32, F), (f32, F))

        def by_tile(v):
            return v.rearrange("p g (t f) -> p g t f", f=F)

        tN, agg, yv, yo, zs_s = (by_tile(v) for v in (tN, agg, yv, yo, zs_s))
        hidT = hidT.rearrange("p g (a c) -> p g a c", a=2)
        yT = hidT[:, :, 1, :]
        bank = [ctx.enter_context(nc.psum_tensor(f"bank{i}", [P, 512], f32)) for i in range(8)]

        clean = sem("clean")
        l_src, l_dst, l_w, l_x, l_par = (sem(n) for n in ("l_src", "l_dst", "l_w", "l_x", "l_par"))
        consts = sem("consts")
        order = sem("order")
        dst_ready, dst_stored = sem("dst_ready"), sem("dst_stored")
        diag_ready, ends_ps, above_ready = sem("diag_ready"), sem("ends_ps"), sem("above_ready")
        chunk_in = [sem(f"chunk_in{i}") for i in range(4)]
        chunk_used = sem("chunk_used")
        end_ready, begin_ps, idx_ready, masks_ready = sem("end_ready"), sem("begin_ps"), sem("idx_ready"), sem("masks_ready")
        x_T, x_Ts, zs_ps, zs_sb = sem("x_T"), sem("x_Ts"), sem("zs_ps"), sem("zs_sb")
        xT_st = [sem(f"xT_st{i}") for i in range(4)]
        zs_st = [sem(f"zs_st{i}") for i in range(4)]
        filled, stepped = sem("filled"), sem("stepped")
        landed = [sem(f"landed{b}") for b in range(NB)]
        dumped = [sem(f"dumped{b}") for b in range(NB)]
        last_T, car_sc, car_T, fix_in, fixed, fix_st = (
            sem(n) for n in ("last_T", "car_sc", "car_T", "fix_in", "fixed", "fix_st"))
        zeroed = [sem("zeroed_low"), sem("zeroed_high")]
        clean_p = sem("clean_p")
        res_in = [sem(f"res_in_{g}") for g in range(NG)]
        grp_in = [[sem(f"grp_in{q}_{i}") for i in range(GB)] for q in range(3)]
        l_edge, l_late, late_free, late_set = (sem(n) for n in ("l_edge", "l_late", "late_free", "late_set"))
        below_ready, pos_ps, from_ready, win_ps, hot_ready, key_ps, lo_ps, key_ready = (
            sem(n) for n in ("below_ready", "pos_ps", "from_ready", "win_ps", "hot_ready", "key_ps", "lo_ps", "key_ready"))
        over_ready, over_ps, large_ready = sem("over_ready"), sem("over_ps"), sem("large_ready")
        made_d, made_sq, made_l = sem("made_d"), sem("made_sq"), sem("made_l")
        paired, added = sem("paired"), sem("added")
        part_in = [sem(f"part_in{i}") for i in range(GB)]
        part_h, part_r, part_m, part_l = (sem(n) for n in ("part_h", "part_r", "part_m", "part_l"))
        adj_ps = [sem(f"adj_ps{q}") for q in range(3)]
        adj_used = [sem(f"adj_used{q}") for q in range(3)]
        grpT_in = [[sem(f"grpT_in{q}_{i}") for i in range(GB)] for q in range(2)]
        zd_ps = sem("zd_ps")
        noted = sem("noted")
        agg_sb = [sem(f"agg_sb{q}") for q in range(3)]
        agg_T = [sem(f"agg_T{q}") for q in range(2)]
        agg_Ts = [sem(f"agg_Ts{q}") for q in range(2)]
        hid_ps = [sem(f"hid_ps{q}") for q in range(2)]
        hid_sb = [sem(f"hid_sb{q}") for q in range(2)]
        o_ps = [sem(f"o_ps{q}") for q in range(2)]
        var_sb = [sem(f"var_sb{q}") for q in range(3)]
        sd_sb = [sem(f"sd_sb{q}") for q in range(3)]
        y_sb = [sem(f"y_sb{q}") for q in range(3)]
        y_st = [[sem(f"y_st{q}_{i}") for i in range(2)] for q in range(3)]
        y_T, y_Ts = sem("y_T"), sem("y_Ts")
        yT_st = [sem(f"yT_st{i}") for i in range(2)]

        block = ctx.enter_context(nc.Block())

        def tiled(table, t, m):
            return table[t * P:(t + m) * P, :].rearrange("(t p) f -> p t f", p=P)

        def run_rows(q):
            return run_d[q][0:ROWS, :].rearrange("(p k) f -> p k f", k=CHUNK)

        def slot(g, j=0):
            return (g % RG) * GT + j

        def taken(n):
            return sum(j in BY_ACT for j in range(n))

        def by_degree(eng, second_layer):
            eng.wait_ge(large_ready, 1)
            is_large = eng.value_load(large[0:1, 0:1], min_val=0, max_val=P)
            with eng.If(is_large):
                second_layer(True)
            with eng.Else():
                second_layer(False)

        @block.sync
        def _(sp):
            def zero_words(at, n):
                return adj_w[:, at:at + n].rearrange("p (a z) -> p a z", z=ZW)

            def repeated(n):
                return zeros[:, :].unsqueeze(1).broadcast_to([P, n // ZW, ZW])

            sp.wait_ge(clean, 1)
            sp.dma_start(xin[:, 0:NT - 1, :], x[0:(NT - 1) * P, :].rearrange("(t p) f -> p t f", p=P)).then_inc(l_x, 16)
            sp.dma_start(xin[0:LASTN, NT - 1, :], x[(NT - 1) * P:N, :]).then_inc(l_x, 16)
            sp.wait_ge(clean, 2)
            sp.dma_start(dst_i[0:FULL, :], dst[0:FULL * CHUNK].rearrange("(p k) -> p k", k=CHUNK)).then_inc(l_dst, 16)
            sp.dma_start(dst_i[FULL:FULL + 1, 0:TAIL], dst[FULL * CHUNK:E].rearrange("(p k) -> p k", p=1)).then_inc(l_dst, 16)
            sp.wait_ge(clean_p, 2)
            for tile, table in ((ed_i, dst), (es_i, src)):
                c0, c1 = (BB - 1) * P * BATCH, (NBATCH - 1) * BATCH
                sp.dma_start(tile[:, 0:BB - 1, :], table[0:c0].rearrange("(c q e) -> q c e", q=P, e=BATCH)).then_inc(l_edge, 16)
                sp.dma_start(tile[0:BLAST - 1, BB - 1, :], table[c0:c1].rearrange("(q e) -> q e", e=BATCH)).then_inc(l_edge, 16)
                sp.dma_start(tile[BLAST - 1:BLAST, BB - 1, 0:E - c1], table[c1:E].rearrange("(q e) -> q e", q=1)).then_inc(l_edge, 16)
            sp.wait_ge(clean_p, 4)
            for tile, table, s in ((src_i, src, l_src), (w_s, w, l_w)):
                sp.dma_start(tile[0:FULL, :], table[0:FULL * CHUNK].rearrange("(p k) -> p k", k=CHUNK)).then_inc(s, 16)
                sp.dma_start(tile[FULL:FULL + 1, 0:TAIL], table[FULL * CHUNK:E].rearrange("(p k) -> p k", p=1)).then_inc(s, 16)
            sp.wait_ge(clean, 3)
            sp.dma_start(zero_words(0, ADJ // 2 - SETUP), repeated(ADJ // 2 - SETUP)).then_inc(zeroed[0], 16)
            sp.wait_ge(dst_ready, 1)
            sp.dma_start(dst_d[:, :], dst_f[:, :]).then_inc(dst_stored, 16)
            for g, (t, m) in enumerate(GROUPS):
                sp.wait_ge(x_Ts, g + 1)
                sp.dma_start(xT_d[:, t * P:(t + m) * P], xT_s[:, g % 4, 0:m * P]).then_inc(xT_st[g % 4], 16)
                sp.wait_ge(zs_sb, g + 1)
                sp.dma_start(tiled(zs_d, t, m), zs_s[:, g % 4, 0:m, :]).then_inc(zs_st[g % 4], 16)

            for i in range(4):
                sp.wait_ge(xT_st[i], 16 * len(range(i, NG, 4)))
                sp.wait_ge(zs_st[i], 16 * len(range(i, NG, 4)))
            sp.wait_ge(dst_stored, 16)
            sp.wait_ge(key_ready, 1)

            def gather_pass(q):
                def turn(i, zero=False):
                    for b in range(NB):
                        if zero and b == 1:
                            sp.dma_start(adj_w[:, bass.ds(i * ZPIECE + (ADJ // 2 - SETUP), ZPIECE)].rearrange(
                                "p (a z) -> p a z", z=ZW), repeated(ZPIECE)).then_inc(zeroed[1], 16)
                        if zero and b == 3:
                            sp.wait_ge(zeroed[1], i * 16 + 16)
                        sp.wait_ge(stepped, q * CHUNK + i * RING + (b + 1) * BS)
                        sp.dma_start(run_rows(q)[:, bass.ds(i * RING + b * BS, BS), :],
                                     runs[:, b * BS:(b + 1) * BS, :]).then_inc(dumped[b], 16)
                if q == 0:
                    with sp.Fori(0, ZROUNDS) as i:
                        turn(i, True)
                with sp.Fori(ZROUNDS if q == 0 else 0, ROUNDS) as i:
                    turn(i)

            def load_group(q, tableT):
                def stage(g):
                    t, m = GROUPS[g]
                    if g >= GB:
                        sp.wait_ge(hid_ps[q], g - GB + 1)
                    sp.dma_start(tT[:, g % GB, 0:m * P], tableT[:, t * P:(t + m) * P]).then_inc(grpT_in[q][g % GB], 16)
                return stage

            def load_rows(q, table):
                def stage(g):
                    t, m = GROUPS[g]
                    if g >= GB:
                        sp.wait_ge(var_sb[q], g - GB + 1)
                    if q == 0 and m + t == NT:
                        sp.dma_start(tN[0:LASTN, g % GB, 0, :], x[t * P:N, :]).then_inc(grp_in[q][g % GB], 16)
                    else:
                        sp.dma_start(tN[:, g % GB, 0:m, :], tiled(table, t, m)).then_inc(grp_in[q][g % GB], 16)
                return stage

            gather_pass(0)
            sp.wait_ge(late_free, 1)
            for tile, table in (
                (w1l[:, :], W1lT), (w1r[:, :], W1rT),
                (w2l[:, :, :], W2lT.rearrange("(a p) f -> p a f", p=P)),
                (w2r[:, :, :], W2rT.rearrange("(a p) f -> p a f", p=P)),
                (w1[:, :, :], W1.rearrange("(a p) f -> p a f", p=P)),
                (w2[:, :], W2), (wd[:, :], Wm[0:F, :]),
            ):
                sp.dma_start(tile, table).then_inc(l_late, 16)
            for i in range(4):
                sp.wait_ge(xT_st[i], 16 * len(range(i, NG, 4)))
                sp.wait_ge(zs_st[i], 16 * len(range(i, NG, 4)))

            def store_x1(g):
                t, m = GROUPS[g]
                sp.wait_ge(y_sb[0], g + 1)
                sp.dma_start(tiled(x1_d, t, m), yo[:, g % 2, 0:m, :]).then_inc(y_st[0][g % 2], 16)

            def store_x1T(g):
                t, m = GROUPS[g]
                sp.wait_ge(y_Ts, g + 1)
                sp.dma_start(x1T_d[:, t * P:(t + m) * P], yT[:, g % 2, 0:m * P]).then_inc(yT_st[g % 2], 16)

            skewed([(0, load_group(0, xT_d)), (3, load_rows(0, x)), (6, store_x1), (7, store_x1T)])

            for i in range(2):
                sp.wait_ge(y_st[0][i], 16 * len(range(i, NG, 2)))
                sp.wait_ge(yT_st[i], 16 * len(range(i, NG, 2)))

            def load_parts(q, table):
                for g, (t, m) in enumerate(GROUPS):
                    if g >= GB or q == 2:
                        sp.wait_ge(part_l, NG * (q - 1) + g - GB + 1)
                    sp.dma_start(tN[:, g % GB, 0:m, :], tiled(table, t, m)).then_inc(part_in[g % GB], 16)
                sp.wait_ge(part_l, NG * q)

            def store_gr(g):
                t, m = GROUPS[g]
                sp.wait_ge(y_sb[1], g + 1)
                sp.dma_start(tiled(g_d, t, m), yo[:, g % 2, 0:m, :]).then_inc(y_st[1][g % 2], 16)
                sp.dma_start(tiled(r_d, t, m), yv[:, g % 2, 0:m, :]).then_inc(y_st[1][g % 2], 16)

            def load_r(g):
                t, m = GROUPS[g]
                if g >= GB:
                    sp.wait_ge(var_sb[2], g - GB + 1)
                sp.dma_start(tN[:, g % GB, 0:m, :], tiled(r_d, t, m)).then_inc(grp_in[2][g % GB], 16)

            def store_out(g):
                t, m = GROUPS[g]
                sp.wait_ge(y_sb[2], g + 1)
                if t + m < NT:
                    sp.dma_start(tiled(out, t, m), yo[:, g % 2, 0:m, :]).then_inc(y_st[2][g % 2], 16)
                else:
                    sp.dma_start(out[t * P:N, :], yo[0:LASTN, g % 2, 0, :]).then_inc(y_st[2][g % 2], 16)

            def second_layer(general):
                if general:
                    gather_pass(1)
                else:
                    load_parts(1, x1_d)
                skewed([(0, load_group(1, x1T_d)), (1, load_rows(1, x1_d)), (5, store_gr)])
                for i in range(2):
                    sp.wait_ge(y_st[1][i], 32 * len(range(i, NG, 2)))
                if general:
                    gather_pass(2)
                else:
                    sp.wait_ge(var_sb[1], NG)
                    load_parts(2, g_d)
                skewed([(0, load_r), (2, store_out)])

            by_degree(sp, second_layer)
            for i in range(2):
                sp.wait_ge(y_st[2][i], 16 * len(range(i, NG, 2)))

        @block.scalar
        def _(act):
            for tile, table in (
                (ws[:, :], Wm[F:2 * F, :]),
                (ww[:, :], Wm[2 * F:2 * F + 1, :].broadcast_to([P, F])),
                (rows[0:1, 0, :], bm.rearrange("(a f) -> a f", a=1)),
                (rows[0:1, 1, :], b2.rearrange("(a f) -> a f", a=1)),
                (rows[0:1, 2, :], b2l.rearrange("(a f) -> a f", a=1)),
                (cols[:, 0:1], b1.rearrange("(p a) -> p a", a=1)),
                (cols[:, 1:2], b1l[0:P].rearrange("(p a) -> p a", a=1)),
                (cols[:, 2:3], b1l[P:2 * P].rearrange("(p a) -> p a", a=1)),
            ):
                act.dma_start(tile, table).then_inc(l_par, 16)

            def copy_zs(g):
                m = GROUPS[g][1]
                act.wait_ge(zs_ps, g + 1)
                if g >= 4:
                    act.wait_ge(zs_st[g % 4], 16 * (g // 4))
                nc.scalar.copy(zs_s[:, g % 4, 0:m, :],
                               bank[2 + g % 2][:, 0:m * P].rearrange("p (t f) -> p t f", f=F)).then_inc(zs_sb, 1)

            for g, (t, m) in enumerate(GROUPS):
                act.wait_ge(x_T, g + 1)
                if g >= 4:
                    act.wait_ge(zs_ps, g - 3)
                    act.wait_ge(xT_st[g % 4], 16 * (g // 4))
                nc.scalar.copy(xT_s[:, g % 4, 0:m * P], bank[g % 2][:, 0:m * P]).then_inc(x_Ts, 1)
                if g:
                    copy_zs(g - 1)
            copy_zs(NG - 1)

            def gather_pass(q):
                def fill(i, b, first):
                    if not first:
                        act.wait_ge(stepped, q * CHUNK + (i - 1) * RING + (b + 1) * BS)
                    last = nc.scalar.copy(idx[:, b * BS:(b + 1) * BS], src_i[:, bass.ds(i * RING + b * BS, BS)])
                    if q == 0:
                        for j in range(BS):
                            last = nc.scalar.activation(gath[:, b * BS + j, :], ww[:, :], ACT.Copy,
                                                        scale=w_s[:, bass.ds(i * RING + b * BS + j, 1)])
                    last.then_inc(filled, 1)

                def turn(i, first, pairs, final=False):
                    for b in range(NB):
                        if b < NB - LEAD:
                            fill(i, b + LEAD, first)
                        elif not final:
                            fill(i + 1, b + LEAD - NB, False)
                        if pairs:
                            mine = [j for j in range(b * BS, min((b + 1) * BS, RP)) if j in BY_ACT]
                            squares(i, mine[0], first)
                            for k, j in enumerate(mine):
                                if k + 1 < len(mine):
                                    squares(i, mine[k + 1], first)
                                low_one_hot(i, j, first)

                def squares(i, j, first):
                    n = taken(j)
                    a = sq[:, n % 2, :]
                    if not (first and n < 2):
                        act.wait_ge(made_l, i * taken(RP) + n - 1)
                    for u in range(SUB):
                        last = nc.scalar.activation(a[:, u * P:(u + 1) * P], iota_l[:, :], ACT.Square,
                                                    bias=nlo[:, u, bass.ds(i * RP + j, 1)])
                    last.then_inc(made_sq, 1)

                def low_one_hot(i, j, first):
                    s, n = j % PR, taken(j)
                    if not (first and j < PR):
                        act.wait_ge(paired, i * RP + j - PR + 1)
                    act.wait_ge(made_sq, i * taken(RP) + n + 1)
                    nc.scalar.activation(hot_l[:, s, :], sq[:, n % 2, :], ACT.Relu, bias=1.0, scale=-1.0).then_inc(made_l, 1)

                for b in range(LEAD):
                    fill(0, b, True)
                if q == 0:
                    act.wait_ge(key_ready, 1)
                turn(0, True, q == 0)
                if q == 0:
                    with act.Fori(1, PROUNDS) as i:
                        turn(i, False, True)
                with act.Fori(PROUNDS if q == 0 else 1, ROUNDS - 1) as i:
                    turn(i, False, False)
                turn(ROUNDS - 1, False, False, final=True)

            def root(q):
                def stage(g):
                    m = GROUPS[g][1]
                    act.wait_ge(var_sb[q], g + 1)
                    if g >= 2:
                        act.wait_ge(y_sb[q], g - 1)
                    nc.scalar.activation(sd[:, g % 2, 0:m], mv[:, g % 2, 0:m, 1], ACT.Sqrt,
                                         bias=eps[:, :]).then_inc(sd_sb[q], 1)
                return stage

            def copy_aggT(q):
                def stage(g):
                    m = GROUPS[g][1]
                    act.wait_ge(agg_T[q], g + 1)
                    if g >= 2:
                        act.wait_ge(hid_ps[q], g - 1)
                    nc.scalar.copy(aggT[:, g % 2, 0:m * P], bank[2][:, 0:m * P]).then_inc(agg_Ts[q], 1)
                return stage

            def relu(q, halves):
                def stage(g):
                    m = GROUPS[g][1]
                    act.wait_ge(hid_ps[q], g + 1)
                    if g >= 2:
                        act.wait_ge(o_ps[q], g - 1)
                    for a in range(halves):
                        last = nc.scalar.activation(hidT[:, g % 2, a, 0:m * P], bank[3 + a][:, 0:m * P], ACT.Relu,
                                                    bias=cols[:, q + a:q + a + 1])
                    last.then_inc(hid_sb[q], 1)
                return stage

            def copy_x1T(g):
                m = GROUPS[g][1]
                act.wait_ge(y_T, g + 1)
                if g >= 2:
                    act.wait_ge(yT_st[g % 2], 16 * (g // 2))
                nc.scalar.copy(yT[:, g % 2, 0:m * P], bank[7][:, 0:m * P]).then_inc(y_Ts, 1)

            act.wait_ge(l_par, 16 * 8)
            act.wait_ge(l_src, 32)
            act.wait_ge(l_w, 32)
            gather_pass(0)
            skewed([(2, copy_aggT(0)), (3, relu(0, 1)), (5, root(0)), (7, copy_x1T)])

            def split(q):
                def high(g):
                    t, m = GROUPS[g]
                    k = (q - 1) * len(range(g % GB, NG, GB)) + g // GB + 1
                    act.wait_ge(part_in[g % GB], 16 * k)
                    nc.scalar.copy(parts[:, t:t + m, 0:F], tN[:, g % GB, 0:m, :]).then_inc(part_h, 1)

                def middle(g):
                    t, m = GROUPS[g]
                    act.wait_ge(part_r, NG * (q - 1) + g + 1)
                    nc.scalar.copy(parts[:, t:t + m, F:2 * F], agg[:, g % 2, 0:m, :]).then_inc(part_m, 1)
                skewed([(0, high), (1, middle)])

            def second_layer(general):
                gather_pass(1) if general else split(1)
                skewed([(2, copy_aggT(1)), (3, relu(1, 2))])
                gather_pass(2) if general else split(2)
                skewed([(1, root(2))])

            by_degree(act, second_layer)

        @block.gpsimd
        def _(pool):
            nc.gpsimd.iota(node_i[:, :], pattern=[[P, NT]], base=0, channel_multiplier=1)
            nc.gpsimd.iota(numbers_i[:, :], pattern=[[P, BB]], base=0, channel_multiplier=1)
            nc.gpsimd.iota(wstart_i[:, :], pattern=[[WIN, WB * P]], base=0, channel_multiplier=0)
            nc.gpsimd.iota(pair_i[:, :], pattern=[[1, PAIRS]], base=0, channel_multiplier=0).then_inc(consts, 1)
            nc.gpsimd.memset(ed_i[:, :, :], int(NODST)).then_inc(clean_p, 1)
            nc.gpsimd.memset(es_i[:, :, :], 0).then_inc(clean_p, 1)
            nc.gpsimd.memset(src_i[:, :], 0).then_inc(clean_p, 1)
            nc.gpsimd.memset(w_s[:, :], 0.0).then_inc(clean_p, 1)
            pool.wait_ge(clean, 4)
            nc.gpsimd.affine_select(out=ident[:, :], in_=ident[:, :], compare_op=ALU.not_equal, fill=1.0, base=0,
                                    pattern=[[-1, P]], channel_multiplier=1).then_inc(consts, 1)
            nc.gpsimd.affine_select(out=shift[:, :], in_=shift[:, :], compare_op=ALU.not_equal, fill=1.0, base=1,
                                    pattern=[[-1, P]], channel_multiplier=1).then_inc(consts, 1)
            nc.gpsimd.affine_select(out=wrap[:, :], in_=wrap[:, :], compare_op=ALU.not_equal, fill=1.0, base=P - 1,
                                    pattern=[[1, P]], channel_multiplier=-1).then_inc(consts, 1)
            pool.wait_ge(above_ready, 1)
            pool.wait_ge(dst_stored, 16)
            for t in range(NT):
                if t >= 4:
                    pool.wait_ge(chunk_used, t - 3)
                pool.indirect_dma_start(chunks[:, t % 4, :], None, dst_d[:, :],
                                        bass.IndirectOffsetOnAxis(ap=above_i[:, t:t + 1], axis=0)).then_inc(chunk_in[t % 4], 16)

            def gather_pass(q, table):
                def turn(i):
                    for b in range(NB):
                        pool.wait_ge(filled, q * ROUNDS * NB + i * NB + b + 1)
                        pool.sem_inc(noted, 1)
                        for j in range(b * BS, (b + 1) * BS):
                            pool.indirect_dma_start(gath[:, j, :], None, table,
                                                    bass.IndirectOffsetOnAxis(ap=idx[:, j:j + 1], axis=0),
                                                    compute_op=ALU.add if q == 0 else ALU.bypass).then_inc(landed[b], 16)
                with pool.Fori(0, ROUNDS) as i:
                    turn(i)
                for b in range(NB):
                    pool.wait_ge(dumped[b], q * ROUNDS * 16 + 16 * ROUNDS)
                pool.wait_ge(idx_ready, 1)
                pool.indirect_dma_start(fix[:, :], None, run_d[q][:, :],
                                        bass.IndirectOffsetOnAxis(ap=idx_fix[:, :], axis=0)).then_inc(fix_in, 16)
                pool.wait_ge(fixed, q + 1)
                pool.indirect_dma_start(run_d[q][:, :], bass.IndirectOffsetOnAxis(ap=idx_fix[:, :], axis=0),
                                        fix[:, :], None).then_inc(fix_st, 16)
                pool.wait_ge(fix_st, 16 * (q + 1))
                for g, (t0, m) in enumerate(GROUPS):
                    if g >= RG:
                        pool.wait_ge(agg_sb[q], g - RG + 1)
                    for t in range(t0, t0 + m):
                        pool.indirect_dma_start(gath[:, slot(g, t - t0), :], None, run_d[q][:, :],
                                                bass.IndirectOffsetOnAxis(ap=idx_end[:, t:t + 1], axis=0)).then_inc(res_in[g], 16)

            for i in range(4):
                pool.wait_ge(zs_st[i], 16 * len(range(i, NG, 4)))
            gather_pass(0, zs_d[:, :])

            def second_layer(general):
                if general:
                    for i in range(2):
                        pool.wait_ge(y_st[0][i], 16 * len(range(i, NG, 2)))
                    gather_pass(1, x1_d[:, :])
                    for i in range(2):
                        pool.wait_ge(y_st[1][i], 32 * len(range(i, NG, 2)))
                    gather_pass(2, g_d[:, :])
                else:
                    pool.nop()

            by_degree(pool, second_layer)

        @block.vector
        def _(dve):
            made = [0]

            def link(ins):
                made[0] += 1
                ins.then_inc(order, 1)
                dve.wait_ge(order, made[0])

            nc.vector.memset(xin[:, NT - 1, :], 0.0).then_inc(clean, 1)
            nc.vector.memset(dst_i[:, :], int(NODST)).then_inc(clean, 1)
            nc.vector.memset(zeros[:, :], 0.0).then_inc(clean, 1)
            nc.vector.memset(ident[:, :], 0.0)
            nc.vector.memset(shift[:, :], 0.0)
            nc.vector.memset(wrap[:, :], 0.0).then_inc(clean, 1)
            nc.vector.memset(ones[:, :], 1.0)
            nc.vector.memset(same[:, 0:1], 0.0)
            nc.vector.memset(cont[:, 0:1], 0.0)
            nc.vector.memset(whole[:, 0:1], 0.0)
            nc.vector.memset(off[:, 0:LAG], 0)
            link(nc.vector.memset(eps[:, :], EPS))

            dve.wait_ge(l_dst, 32)
            nc.vector.tensor_copy(dst_f[:, :], dst_i[:, :]).then_inc(dst_ready, 1)
            dve.wait_ge(dst_ready, 1)
            dve.wait_ge(consts, 4)
            nc.vector.tensor_scalar(diag[:, 0, :], ident[:, :], dst_f[:, 0:1], None, ALU.mult)
            nc.vector.tensor_scalar(diag[:, 1, :], ident[:, :], dst_f[:, CHUNK - 1:CHUNK], None, ALU.mult).then_inc(diag_ready, 1)
            nc.vector.tensor_copy(node[:, :], node_i[:, :])
            nc.vector.tensor_copy(numbers[:, :], numbers_i[:, :])
            nc.vector.tensor_copy(wstart[:, :], wstart_i[:, :])
            nc.vector.tensor_copy(pair[:, :], pair_i[:, :])
            nc.vector.tensor_copy(iota_d[:, :], pair_i[:, 0:COLS])
            nc.vector.tensor_copy(iota_l[:, :], pair_i[:, 0:P])
            nc.vector.tensor_scalar(niota_l[:, :], pair_i[:, 0:P], -1.0, None, ALU.mult)
            link(nc.vector.tensor_tensor(same[:, 1:CHUNK], dst_f[:, 1:CHUNK], dst_f[:, 0:CHUNK - 1], ALU.is_equal))
            link(nc.vector.tensor_scalar(keep[:, :], same[:, :], 2 * BIG, -BIG, ALU.mult, ALU.add))
            dve.wait_ge(ends_ps, 1)
            link(nc.vector.tensor_copy(ends[:, :, :], bank[4][:, 0:2 * P].rearrange("p (a c) -> p a c", a=2)))
            for t in range(NT):
                part = t % (CHUNK // P) * P
                last = nc.vector.tensor_scalar(junk[:, part:part + P], ends[:, 1, :], node[:, t:t + 1], None,
                                               ALU.is_le, ALU.add, accum_out=above[:, t:t + 1])
                if part + 2 * P > CHUNK or t == NT - 1:
                    link(last)
            nc.vector.tensor_copy(above_i[:, :], above[:, :]).then_inc(above_ready, 1)
            nc.vector.tensor_tensor(cont[:, 1:P], ends[:, 0, 1:P], ends[:, 1, 0:P - 1], ALU.is_equal)
            link(nc.vector.tensor_tensor(whole[:, 1:P], ends[:, 0, 0:P - 1], ends[:, 1, 0:P - 1], ALU.is_equal))
            nc.vector.tensor_copy(mb[:, 1, :], cont[:, :])
            link(nc.vector.tensor_tensor(ma[:, 1, :], cont[:, :], whole[:, :], ALU.mult))
            nc.vector.tensor_scalar(mb[:, 0, :], cont[:, :], 2 * BIG, -BIG, ALU.mult, ALU.add)
            link(nc.vector.tensor_scalar(ma[:, 0, :], ma[:, 1, :], 2 * BIG, -BIG, ALU.mult, ALU.add))

            dve.wait_ge(l_edge, 96)
            nc.vector.tensor_copy(ed_f[:, :, :], ed_i[:, :, :])
            nc.vector.tensor_scalar(eh_i[:, :, :], es_i[:, :, :], 7, None, ALU.logical_shift_right)
            link(nc.vector.tensor_scalar(el_i[:, :, :], es_i[:, :, :], P - 1, None, ALU.bitwise_and))
            for c in range(BB):
                last = nc.vector.tensor_scalar(below[:, c, :], wstart[:, :], ed_f[:, c, BATCH - 1:BATCH], None, ALU.is_gt)
            last.then_inc(below_ready, 1)
            nc.vector.tensor_copy(eh_f[:, :, :], eh_i[:, :, :])
            nc.vector.tensor_scalar(el_f[:, :, :], el_i[:, :, :], -1.0, None, ALU.mult)
            link(nc.vector.tensor_scalar(tmp[:, 0, 0:WB], numbers[:, 0:WB], float(NWIN), 1e6, ALU.is_ge, ALU.mult))
            nc.vector.scalar_tensor_tensor(ek[:, :, :], ed_f[:, :, :], float(NT), eh_f[:, :, :], ALU.mult, ALU.add)
            link(nc.vector.tensor_tensor(tmp[:, 1, 0:WB], tmp[:, 0, 0:WB], numbers[:, 0:WB], ALU.add))
            dve.wait_ge(pos_ps, 1)
            link(nc.vector.tensor_tensor(pos[:, :], tmp[:, 1, 0:WB], bank[4][:, 256:256 + WB], ALU.add))
            for c in range(WB):
                last = nc.vector.tensor_scalar(from_pos[:, c, :], pair[:, :], pos[:, c:c + 1], None, ALU.is_ge)
            last.then_inc(from_ready, 1)
            dve.wait_ge(win_ps, 1)
            for a in range(2):
                k = min(HALF, PAIRS - a * HALF)
                last = nc.vector.tensor_scalar(win[:, a * HALF:a * HALF + k], bank[5 + a][:, 0:k], -1.0, None, ALU.add)
            link(last)
            nc.vector.tensor_scalar(off[:, LAG:LAG + PAIRS], win[:, :], float(COLS), None, ALU.mult)
            link(nc.vector.tensor_tensor(batch[:, :], pair[:, :], win[:, :], ALU.subtract))
            for c in range(BB):
                last = nc.vector.tensor_scalar(hot[:, c, :], batch[:, :], numbers[:, c:c + 1], None, ALU.is_equal)
            last.then_inc(hot_ready, 1)
            for t in range(NT):
                dve.wait_ge(chunk_in[t % 4], 16 * (t // 4 + 1))
                nc.vector.tensor_scalar(junk[:, :], chunks[:, t % 4, :], node[:, t:t + 1], None, ALU.is_le, ALU.add,
                                        accum_out=cnt[:, t:t + 1]).then_inc(chunk_used, 1)
                dve.wait_ge(chunk_used, t + 1)
            nc.vector.tensor_scalar(junk[:, :], dst_f[:, :], dst_f[:, 0:1], None, ALU.is_equal, ALU.add, accum_out=over[:, 0:1])
            nc.vector.scalar_tensor_tensor(end[:, :], above[:, :], float(CHUNK), cnt[:, :], ALU.mult, ALU.add).then_inc(end_ready, 1)
            dve.wait_ge(end_ready, 1)
            link(nc.vector.scalar_tensor_tensor(over[:, 1:2], numbers[:, 0:1], float(CHUNK), over[:, 0:1], ALU.mult, ALU.add))
            nc.vector.tensor_scalar(idx_fix[:, :], over[:, 1:2], -1.0, None, ALU.add)
            link(nc.vector.tensor_scalar(tmp[:, 1, :], end[:, :], -1.0, 0.0, ALU.add, ALU.max))
            dve.wait_ge(begin_ps, 1)
            link(nc.vector.tensor_copy(begin[:, :], bank[4][:, 400:400 + NT]))
            nc.vector.tensor_copy(idx_end[:, :], tmp[:, 1, :])
            link(nc.vector.tensor_tensor(tmp[:, 2, :], end[:, :], begin[:, :], ALU.subtract))
            nc.vector.tensor_scalar(has[:, :], tmp[:, 2, :], 0.0, None, ALU.is_gt)
            link(nc.vector.tensor_scalar(tmp[:, 3, :], tmp[:, 2, :], 1.0, None, ALU.max))
            link(nc.vector.reciprocal(tmp[:, 0, :], tmp[:, 3, :]))
            nc.vector.tensor_tensor(scale[:, :], tmp[:, 0, :], has[:, :], ALU.mult).then_inc(idx_ready, 1)
            degree = tmp[:, 2, :]
            link(nc.vector.tensor_reduce(over[:, 0:1], degree, mybir.AxisListType.X, ALU.max))
            nc.vector.tensor_scalar(over[:, 1:2], over[:, 0:1], float(DENSE_MAX), None, ALU.is_gt).then_inc(over_ready, 1)
            dve.wait_ge(over_ps, 1)
            nc.vector.tensor_copy(large[:, :], bank[5][:, 400:401]).then_inc(large_ready, 1)

            dve.wait_ge(lo_ps, 1)
            for u in range(SUB):
                for a in range(2):
                    k, h = min(HALF, PAIRS - a * HALF), a * HALF
                    nc.vector.scalar_tensor_tensor(key[:, u, h:h + k], win[:, h:h + k], -float(COLS),
                                                   bank[2 * u + a][:, 0:k], ALU.mult, ALU.add)
                    last = nc.vector.tensor_copy(nlo[:, u, h:h + k], bank[4 + 2 * u + a][:, 0:k])
            last.then_inc(key_ready, 1)
            dve.wait_ge(key_ready, 1)
            def gather_pass(q):
                op0, op1 = (ALU.min, ALU.max) if q == 0 else (ALU.mult, ALU.add)
                mask = keep if q == 0 else same
                v = 0 if q == 0 else 1
                link(nc.vector.memset(runs[:, RING - 1, :], 0.0))

                def turn(i, first, pairs):
                    offs = []
                    for b in range(NB):
                        dve.wait_ge(landed[b], q * ROUNDS * BS * 16 + 16 * BS * i + 16 * BS)
                        if not first:
                            dve.wait_ge(dumped[b], q * ROUNDS * 16 + 16 * i)
                        for j in range(b * BS, (b + 1) * BS):
                            if pairs and j < RP and j % OFFS == 0:
                                offs += nc.values_load_multi_w_load_instructions(
                                    off[0:1, bass.ds(i * RP + j, OFFS)], engines=[mybir.EngineType.DVE],
                                    min_val=0, max_val=(NWIN - 1) * COLS, skip_runtime_bounds_check_because=WINDOWS)[1]
                            if not (first and j == 0):
                                dve.wait_ge(stepped, q * CHUNK + i * RING + j)
                            nc.vector.scalar_tensor_tensor(
                                runs[:, j, :], runs[:, (j - 1) % RING, :], mask[:, bass.ds(i * RING + j, 1)],
                                gath[:, j, :], op0, op1).then_inc(stepped, 1)
                            if pairs and j < RP:
                                one_hots(i, j, first)
                                if not (first and j < LAG):
                                    add_product(offs[j], i * RP + j - LAG, (j - LAG) % PR, first and j == LAG)

                def one_hots(i, j, first):
                    s = j % PR
                    if not (first and j < PR):
                        dve.wait_ge(paired, i * RP + j - PR + 1)
                    for u in range(SUB):
                        if j not in BY_ACT:
                            nc.vector.tensor_scalar(hot_l[:, s, u * P:(u + 1) * P], niota_l[:, :],
                                                    nlo[:, u, bass.ds(i * RP + j, 1)], None, ALU.is_equal)
                        last = nc.vector.tensor_scalar(hot_d[:, s, u * COLS:(u + 1) * COLS], iota_d[:, :],
                                                       key[:, u, bass.ds(i * RP + j, 1)], None, ALU.is_equal)
                    last.then_inc(made_d, 1)

                def add_product(at, n, s, alone):
                    dve.wait_ge(paired, n + 1)
                    if not alone:
                        dve.wait_ge(added, n)
                    a = adj[:, bass.ds(at, COLS)]
                    nc.vector.tensor_tensor(a, bank[s][:, 0:COLS], a, ALU.add).then_inc(added, 1)

                if q == 0:
                    dve.wait_ge(zeroed[0], 16)
                turn(0, True, q == 0)
                if q == 0:
                    with dve.Fori(1, SAFE) as i:
                        turn(i, False, True)
                    with dve.Fori(SAFE, SAFE + ZROUNDS) as i:
                        dve.wait_ge(zeroed[1], i * 16 - (SAFE - 1) * 16)
                        turn(i, False, True)
                    with dve.Fori(SAFE + ZROUNDS, PROUNDS) as i:
                        turn(i, False, True)
                    offs = nc.values_load_multi_w_load_instructions(
                        off[0:1, PAIRS:PAIRS + LAG], engines=[mybir.EngineType.DVE], min_val=0,
                        max_val=(NWIN - 1) * COLS, skip_runtime_bounds_check_because=WINDOWS)[1]
                    for k in range(LAG):
                        add_product(offs[k], PAIRS - LAG + k, (PAIRS - LAG + k) % PR, False)
                with dve.Fori(PROUNDS if q == 0 else 1, ROUNDS) as i:
                    turn(i, False, False)
                if q == 0:
                    dve.wait_ge(added, PAIRS)
                    link(nc.vector.memset(tN[:, :, :, :], 0.0))
                    nc.vector.memset(agg[:, :, :, :], 0.0).then_inc(late_free, 1)
                dve.wait_ge(last_T, q + 1)
                nc.vector.memset(carry[:, 0, 0:1], -BIG if q == 0 else 0.0)
                link(nc.vector.tensor_tensor(carry[:, 0, 1:P], bank[4][:, 0:P - 1], mb[:, v, 1:P], op0))
                nc.vector.tensor_tensor_scan(carry[:, 1, :], ma[:, v, :], carry[:, 0, :], 0.0, op0, op1).then_inc(car_sc, 1)
                dve.wait_ge(car_T, q + 1)
                dve.wait_ge(fix_in, 16 * (q + 1))
                nc.vector.tensor_tensor(fix[:, :], fix[:, :], bank[5][:, 0:F], op1).then_inc(fixed, 1)

            def joined(q, g):
                dve.wait_ge(res_in[g], 16 * GROUPS[g][1] * (q + 1))

            def per_node(v, t, m):
                return v[:, t:t + m].unsqueeze(2).broadcast_to([P, m, F])

            def join0(g):
                t, m = GROUPS[g]
                joined(0, g)
                dve.wait_ge(zd_ps, g + 1)
                if g >= 2:
                    dve.wait_ge(agg_T[0], g - 1)
                a = agg[:, g % 2, 0:m, :]
                link(nc.vector.tensor_tensor(a, gath[:, slot(g):slot(g) + m, :],
                                             bank[g % 2][:, 0:m * P].rearrange("p (t f) -> p t f", f=F), ALU.add))
                nc.vector.tensor_tensor(a, a, per_node(has, t, m), ALU.mult).then_inc(agg_sb[0], 1)

            def stats(q, g):
                m = GROUPS[g][1]
                for j in range(m):
                    last = nc.vector.bn_stats(st[:, g % 2, j, :], yv[:, g % 2, j, :])
                link(last)
                for j in range(m):
                    last = nc.vector.bn_aggr(mv[:, g % 2, j, :], st[:, g % 2, j, :])
                last.then_inc(var_sb[q], 1)

            def residual0(g):
                m = GROUPS[g][1]
                dve.wait_ge(o_ps[0], g + 1)
                dve.wait_ge(grp_in[0][g % GB], 16 * (g // GB + 1))
                if g >= 2:
                    dve.wait_ge(y_sb[0], g - 1)
                link(nc.vector.tensor_tensor(yv[:, g % 2, 0:m, :], bank[5 + g % 2][:, 0:m * P].rearrange("p (t f) -> p t f", f=F),
                                             tN[:, g % GB, 0:m, :], ALU.add))
                stats(0, g)

            def norm(q):
                def stage(g):
                    m = GROUPS[g][1]
                    dve.wait_ge(sd_sb[q], g + 1)
                    if g >= 2:
                        dve.wait_ge(y_st[q][g % 2], 16 * (g // 2))
                        if q == 0:
                            dve.wait_ge(y_T, g - 1)
                    link(nc.vector.reciprocal(rs[:, g % 2, 0:m], sd[:, g % 2, 0:m]))
                    for j in range(m):
                        last = nc.vector.tensor_scalar(yo[:, g % 2, j, :], yv[:, g % 2, j, :], mv[:, g % 2, j, 0:1],
                                                       rs[:, g % 2, j:j + 1], ALU.subtract, ALU.mult)
                    last.then_inc(y_sb[q], 1)
                return stage

            def join1(g):
                t, m = GROUPS[g]
                joined(1, g)
                if g >= 2:
                    dve.wait_ge(agg_T[1], g - 1)
                nc.vector.tensor_tensor(agg[:, g % 2, 0:m, :], gath[:, slot(g):slot(g) + m, :],
                                        per_node(scale, t, m), ALU.mult).then_inc(agg_sb[1], 1)

            def take1(g):
                m = GROUPS[g][1]
                dve.wait_ge(o_ps[1], g + 1)
                dve.wait_ge(grp_in[1][g % GB], 16 * (g // GB + 1))
                if g >= 2:
                    dve.wait_ge(y_st[1][g % 2], 32 * (g // 2))
                nc.vector.tensor_copy(yo[:, g % 2, 0:m, :], bank[5][:, 0:m * P].rearrange("p (t f) -> p t f", f=F))
                nc.vector.tensor_tensor(yv[:, g % 2, 0:m, :], bank[6][:, 0:m * P].rearrange("p (t f) -> p t f", f=F),
                                        tN[:, g % GB, 0:m, :], ALU.add).then_inc(y_sb[1], 1)
                dve.wait_ge(y_sb[1], g + 1)
                nc.vector.memset(st[:, g % 2, 0, 0:1], 0.0).then_inc(var_sb[1], 1)

            def join2(g):
                t, m = GROUPS[g]
                joined(2, g)
                dve.wait_ge(grp_in[2][g % GB], 16 * (g // GB + 1))
                if g >= 2:
                    dve.wait_ge(y_sb[2], g - 1)
                nc.vector.tensor_copy(agg[:, g % 2, 0:m, :], gath[:, slot(g):slot(g) + m, :]).then_inc(agg_sb[2], 1)
                dve.wait_ge(agg_sb[2], g + 1)
                residual2(g)

            def residual2(g):
                t, m = GROUPS[g]
                for j in range(m):
                    last = nc.vector.scalar_tensor_tensor(yv[:, g % 2, j, :], agg[:, g % 2, j, :], scale[:, t + j:t + j + 1],
                                                          tN[:, g % GB, j, :], ALU.mult, ALU.add)
                link(last)
                stats(2, g)



            gather_pass(0)
            skewed([(1, join0), (5, residual0), (6, norm(0))])

            def split(q):
                def rest(g):
                    t, m = GROUPS[g]
                    dve.wait_ge(part_h, NG * (q - 1) + g + 1)
                    if g >= 2:
                        dve.wait_ge(part_l, NG * (q - 1) + g - 1)
                    nc.vector.tensor_tensor(agg[:, g % 2, 0:m, :], tN[:, g % GB, 0:m, :], parts[:, t:t + m, 0:F],
                                            ALU.subtract).then_inc(part_r, 1)

                def low(g):
                    t, m = GROUPS[g]
                    dve.wait_ge(part_m, NG * (q - 1) + g + 1)
                    nc.vector.tensor_tensor(parts[:, t:t + m, 2 * F:3 * F], agg[:, g % 2, 0:m, :],
                                            parts[:, t:t + m, F:2 * F], ALU.subtract).then_inc(part_l, 1)
                skewed([(0, rest), (1, low)])

            def three_parts(q, g):
                t, m = GROUPS[g]
                if q == 1 and g >= 2:
                    dve.wait_ge(agg_T[1], g - 1)
                if q == 2 and g >= 2:
                    dve.wait_ge(y_sb[2], g - 1)
                for j in range(m):
                    dve.wait_ge(adj_ps[q], t + j + 1)
                    k, o = (LASTM if t + j == NT - 1 else P), bank[ADJ_BANKS[(t + j) % 3]]
                    nc.vector.tensor_reduce(agg[0:k, g % 2, j, :], o[0:k, 0:3 * F].rearrange("p (a f) -> p f a", a=3),
                                            mybir.AxisListType.X, ALU.add).then_inc(adj_used[q], 1)
                dve.wait_ge(adj_used[q], t + m)

            def mean1(g):
                t, m = GROUPS[g]
                three_parts(1, g)
                a = agg[:, g % 2, 0:m, :]
                nc.vector.tensor_tensor(a, a, per_node(scale, t, m), ALU.mult).then_inc(agg_sb[1], 1)

            def mean2(g):
                t, m = GROUPS[g]
                dve.wait_ge(grp_in[2][g % GB], 16 * (g // GB + 1))
                three_parts(2, g)
                residual2(g)

            before = made[0]

            def second_layer(general):
                made[0] = before
                if general:
                    link(nc.vector.tensor_scalar(same[:, :], keep[:, :], 0.0, None, ALU.is_gt))
                gather_pass(1) if general else split(1)
                skewed([(1, join1 if general else mean1), (4, take1)])
                gather_pass(2) if general else split(2)
                skewed([(1, join2 if general else mean2), (2, norm(2))])

            by_degree(dve, second_layer)

        @block.tensor
        def _(pe):
            pe.wait_ge(diag_ready, 1)
            for a in range(2):
                last = nc.tensor.matmul(bank[4][:, a * P:(a + 1) * P], ones[:, :], diag[:, a, :], start=True, stop=True)
            last.then_inc(ends_ps, 1)
            pe.wait_ge(below_ready, 1)
            for a in range(WB):
                for c in range(BB):
                    last = nc.tensor.matmul(bank[4][:, 256 + a:257 + a], below[:, c, a * P:(a + 1) * P], ones[:, 0:1],
                                            start=c == 0, stop=c == BB - 1)
            last.then_inc(pos_ps, 1)
            pe.wait_ge(l_x, 32)
            pe.wait_ge(l_par, 16 * 8)
            for g in range(NG + 1):
                if g == 3:
                    pe.wait_ge(from_ready, 1)
                    for a in range(2):
                        k = min(HALF, PAIRS - a * HALF)
                        for c in range(WB):
                            last = nc.tensor.matmul(bank[5 + a][:, 0:k], ones[:, :], from_pos[:, c, a * HALF:a * HALF + k],
                                                    start=c == 0, stop=c == WB - 1)
                    last.then_inc(win_ps, 1)
                if g < NG:
                    t, m = GROUPS[g]
                    if g >= 2:
                        pe.wait_ge(x_Ts, g - 1)
                    for j in range(m):
                        last = nc.tensor.transpose(bank[g % 2][:, j * P:(j + 1) * P], xin[:, t + j, :], ident[:, :])
                    last.then_inc(x_T, 1)
                if g:
                    h, (t, m) = g - 1, GROUPS[g - 1]
                    pe.wait_ge(x_Ts, h + 1)
                    if h >= 2:
                        pe.wait_ge(zs_sb, h - 1)
                    for j in range(m):
                        last = nc.tensor.matmul(bank[2 + h % 2][:, j * P:(j + 1) * P], xT_s[:, h % 4, j * P:(j + 1) * P],
                                                ws[:, :], start=True, stop=True)
                    last.then_inc(zs_ps, 1)
            pe.wait_ge(hot_ready, 1)
            pe.wait_ge(zs_sb, NG)
            for u in range(SUB):
                for what, b in ((ek, 2 * u), (el_f, 4 + 2 * u)):
                    for a in range(2):
                        k = min(HALF, PAIRS - a * HALF)
                        for c in range(BB):
                            last = nc.tensor.matmul(bank[b + a][:, 0:k], what[:, c, u * P:(u + 1) * P],
                                                    hot[:, c, a * HALF:a * HALF + k], start=c == 0, stop=c == BB - 1)
            last.then_inc(lo_ps, 1)

            pe.wait_ge(end_ready, 1)
            nc.tensor.matmul(bank[4][:, 400:400 + NT], shift[:, :], end[:, :], start=True, stop=False)
            nc.tensor.matmul(bank[4][:, 401:400 + NT], wrap[:, :], end[:, 0:NT - 1], start=False, stop=True).then_inc(begin_ps, 1)

            pe.wait_ge(over_ready, 1)
            nc.tensor.matmul(bank[5][:, 400:401], ones[:, :], over[:, 1:2], start=True, stop=True).then_inc(over_ps, 1)
            pe.wait_ge(key_ready, 1)

            def pairs(i, first):
                for j in range(RP):
                    s = j % PR
                    if j in BY_ACT:
                        pe.wait_ge(made_l, i * taken(RP) + taken(j) + 1)
                    pe.wait_ge(made_d, i * RP + j + 1)
                    if not (first and j < PR):
                        pe.wait_ge(added, i * RP + j - PR + 1)
                    for u in range(SUB):
                        last = nc.tensor.matmul(bank[s][:, 0:COLS], hot_l[:, s, u * P:(u + 1) * P],
                                                hot_d[:, s, u * COLS:(u + 1) * COLS], start=u == 0, stop=u == SUB - 1)
                    last.then_inc(paired, 1)

            pairs(0, True)
            with pe.Fori(1, PROUNDS) as i:
                pairs(i, False)
            pe.wait_ge(added, PAIRS)

            def carries(q):
                pe.wait_ge(stepped, q * CHUNK + CHUNK)
                nc.tensor.transpose(bank[4][:, 0:P], runs[:, RING - 1, :], ident[:, :]).then_inc(last_T, 1)
                pe.wait_ge(car_sc, q + 1)
                nc.tensor.transpose(bank[5][:, 0:P], carry[:, 1, :], ident[:, :]).then_inc(car_T, 1)

            def product_zd(g):
                m = GROUPS[g][1]
                pe.wait_ge(grpT_in[0][g % GB], 16 * (g // GB + 1))
                if g >= 2:
                    pe.wait_ge(agg_sb[0], g - 1)
                for j in range(m):
                    o = bank[g % 2][:, j * P:(j + 1) * P]
                    nc.tensor.matmul(o, tT[:, g % GB, j * P:(j + 1) * P], wd[:, :], start=True, stop=False)
                    last = nc.tensor.matmul(o, ones[0:1, :], rows[0:1, 0, :], start=False, stop=True)
                last.then_inc(zd_ps, 1)

            def agg_transposed(q):
                def stage(g):
                    m = GROUPS[g][1]
                    pe.wait_ge(agg_sb[q], g + 1)
                    if g >= 1:
                        pe.wait_ge(agg_Ts[q], g)
                    for j in range(m):
                        last = nc.tensor.transpose(bank[2][:, j * P:(j + 1) * P], agg[:, g % 2, j, :], ident[:, :])
                    last.then_inc(agg_T[q], 1)
                return stage

            def hidden(q, wa, wb, halves):
                def stage(g):
                    m = GROUPS[g][1]
                    pe.wait_ge(agg_Ts[q], g + 1)
                    pe.wait_ge(grpT_in[q][g % GB], 16 * (g // GB + 1))
                    if g >= 1:
                        pe.wait_ge(hid_sb[q], g)
                    for a in range(halves):
                        o = bank[3 + a][:, 0:m * P]
                        nc.tensor.matmul(o, wa[:, a * P:(a + 1) * P], tT[:, g % GB, 0:m * P], start=True, stop=False)
                        last = nc.tensor.matmul(o, wb[:, a * P:(a + 1) * P], aggT[:, g % 2, 0:m * P], start=False, stop=True)
                    last.then_inc(hid_ps[q], 1)
                return stage

            def out0(g):
                m = GROUPS[g][1]
                pe.wait_ge(hid_sb[0], g + 1)
                if g >= 2:
                    pe.wait_ge(var_sb[0], g - 1)
                for j in range(m):
                    o = bank[5 + g % 2][:, j * P:(j + 1) * P]
                    nc.tensor.matmul(o, hidT[:, g % 2, 0, j * P:(j + 1) * P], w2[:, :], start=True, stop=False)
                    last = nc.tensor.matmul(o, ones[0:1, :], rows[0:1, 1, :], start=False, stop=True)
                last.then_inc(o_ps[0], 1)

            def x1_transposed(g):
                m = GROUPS[g][1]
                pe.wait_ge(y_sb[0], g + 1)
                if g >= 1:
                    pe.wait_ge(y_Ts, g)
                for j in range(m):
                    last = nc.tensor.transpose(bank[7][:, j * P:(j + 1) * P], yo[:, g % 2, j, :], ident[:, :])
                last.then_inc(y_T, 1)

            def out1(g):
                m = GROUPS[g][1]
                pe.wait_ge(hid_sb[1], g + 1)
                if g >= 1:
                    pe.wait_ge(y_sb[1], g)
                for j in range(m):
                    for o, wt in ((bank[5][:, j * P:(j + 1) * P], w2l), (bank[6][:, j * P:(j + 1) * P], w2r)):
                        for a in range(2):
                            last = nc.tensor.matmul(o, hidT[:, g % 2, a, j * P:(j + 1) * P], wt[:, a, :],
                                                    start=a == 0, stop=a == 1 and wt is w2l)
                        if wt is w2r:
                            last = nc.tensor.matmul(o, ones[0:1, :], rows[0:1, 2, :], start=False, stop=True)
                last.then_inc(o_ps[1], 1)

            def adjacent(q):
                def stage(g):
                    t0, m = GROUPS[g]
                    if g == 0:
                        for h in range(NT):
                            if h % GT == 0:
                                pe.wait_ge(part_l, NG * (q - 1) + h // GT + 1)
                            for t in range(m):
                                last = product(t, h)
                                if h == NT - 1:
                                    last.then_inc(adj_ps[q], 1)
                        return
                    for t in range(t0, t0 + m):
                        if t >= 3:
                            pe.wait_ge(adj_used[q], t - 2)
                        for h in range(NT):
                            last = product(t, h)
                        last.then_inc(adj_ps[q], 1)

                def product(t, h):
                    k = LASTM if t == NT - 1 else P
                    return nc.tensor.matmul(bank[ADJ_BANKS[t % 3]][0:k, 0:3 * F], adj_v[:, t * P:t * P + k, h],
                                            parts[:, h, :], start=h == 0, stop=h == NT - 1)
                return stage

            carries(0)
            pe.wait_ge(l_late, 16 * 7)
            w1f = w1[:, :, :].rearrange("p a f -> p (a f)")
            skewed([(0, product_zd), (2, agg_transposed(0)), (3, hidden(0, w1f[:, 0:F], w1f[:, F:2 * F], 1)),
                    (4, out0), (7, x1_transposed)])

            def second_layer(general):
                layer = [(2, agg_transposed(1)), (3, hidden(1, w1r, w1l, 2)), (4, out1)]
                if general:
                    carries(1)
                    skewed(layer)
                    carries(2)
                else:
                    skewed([(0, adjacent(1)), *layer])
                    skewed([(0, adjacent(2))])

            by_degree(pe, second_layer)


_INS = ["x", "src", "dst", "edge_weight", "L0_gnn_Wm", "L0_gnn_bm", "L0_gnn_W1", "L0_gnn_b1", "L0_gnn_W2", "L0_gnn_b2",
        "L1_gnn_W1l", "L1_gnn_b1l", "L1_gnn_W1r", "L1_gnn_W2l", "L1_gnn_b2l", "L1_gnn_W2r"]
_TRANSPOSED = ["L1_gnn_W1l", "L1_gnn_W1r", "L1_gnn_W2l", "L1_gnn_W2r"]


def kernel(**inputs):
    import numpy as np
    import concourse.bacc as bacc
    from concourse import mybir as _mybir
    from concourse.bass_utils import run_bass_kernel_spmd as run

    nc = bacc.Bacc("TRN2", target_bir_lowering=False, num_devices=1, dynamic_dma_scratch_size=8192)
    arrays, args = {}, []
    for name in _INS:
        a = np.asarray(inputs[name])
        a = np.ascontiguousarray(a.T if name in _TRANSPOSED else a)
        arrays[f"in_{name}_dram"] = a
        args.append(nc.dram_tensor(f"in_{name}_dram", a.shape, _mybir.dt.from_np(a.dtype), kind="ExternalInput").ap())
    args.append(nc.dram_tensor("out_0_dram", (N, F), _mybir.dt.float32, kind="ExternalOutput").ap())
    gnn_kernel(nc, *args)
    r = run(nc, [arrays], core_ids=[0])
    return r.results[0]["out_0_dram"]
```
